# Optimizing a Trainium2 kernel written in Bass

```python
import numpy as np
import jax
import jax.numpy as jnp

def _softmax(x, axis=-1):
    return jax.nn.softmax(x, axis=axis)

def _gelu(x):
    return jax.nn.gelu(x, approximate=True)

def _silu(x):
    return jax.nn.silu(x)

def _sigmoid(x):
    return jax.nn.sigmoid(x)

def _layernorm(x, axis=-1, eps=1e-05):
    m = jnp.mean(x, axis=axis, keepdims=True)
    v = jnp.var(x, axis=axis, keepdims=True)
    return (x - m) / jnp.sqrt(v + eps)

def _scatter_add(tgt, idx, src, axis=0):
    return tgt.at[idx].add(src)

def _segment_sum(src, seg, n):
    return jax.ops.segment_sum(src, seg, n)
kernel_name = 'mk_adj_ffn_d1_adj_r2_20ecc3'

def setup_inputs(seed: int=0):
    np.random.seed(seed)
    _w = jnp.asarray

    def _rec_inputs():
        import jax
        import jax.numpy as jnp
        _gk = jax.random.key(seed)
        x = -0.0005207 + 1.001 * jax.random.normal(jax.random.fold_in(_gk, 1), (128, 128, 128), jnp.float32)
        _w = (1.0 + jnp.arange(128, dtype=jnp.float32)) ** (-0.5)
        _w = _w / _w.mean()
        _pij = jnp.clip(0.03125 * _w[:, None] * _w[None, :], 0.0, 1.0)
        _a = jax.random.uniform(jax.random.fold_in(_gk, 2), (128, 128, 128)) < _pij
        _a = jnp.logical_or(_a, jnp.swapaxes(_a, -1, -2))
        _a = jnp.logical_or(_a, jnp.eye(128, dtype=bool))
        _af = _a.astype(jnp.float32)
        _af = _af * jax.random.uniform(jax.random.fold_in(_gk, 3), (128, 128, 128), jnp.float32, 0.05, 1)
        adj = _af
        return (x, adj)
    x, adj = _rec_inputs()

    def _L0_gnn_setup():
        import jax, jax.numpy as jnp
        import numpy as np
        EPS = 1e-07
        key = jax.random.key(seed)
        k1, k2, k3, k4, k5 = jax.random.split(key, 5)
        B, L, D, U = (8, 512, 128, 128)
        seq_data = jax.random.normal(k1, (B, L, D), dtype=jnp.float32)
        graph = jax.random.uniform(k2, (B, L, L), dtype=jnp.float32)
        scale = 1.0 / np.sqrt(D)
        e_weight = jax.random.normal(k3, (D, U), dtype=jnp.float32) * scale
        Wx = jax.random.normal(k4, (U, U), dtype=jnp.float32) * scale
        Wh = jax.random.normal(k5, (U, U), dtype=jnp.float32) * scale
        b = jnp.zeros((U,), dtype=jnp.float32)
        return {'seq_data': seq_data, 'graph': graph, 'e_weight': e_weight, 'Wx': Wx, 'Wh': Wh, 'b': b}
    _L0_gnn_all = _L0_gnn_setup()
    _L0_gnn_in = {k: v for k, v in _L0_gnn_all.items() if k in ('e_weight', 'Wx', 'Wh', 'b')}
    del _L0_gnn_all

    def _L0_ffn_setup():
        import jax, jax.numpy as jnp
        import numpy as np
        B, S, H, F, E, K = (8, 2048, 128, 256, 16, 2)
        EPS = 1e-05
        key = jax.random.key(seed)
        ks = jax.random.split(key, 9)
        sc = 0.02
        return {'x': jax.random.normal(ks[0], (B, S, H), dtype=jnp.float32), 'gate_w': jax.random.normal(ks[1], (H, E), dtype=jnp.float32) * sc, 'gate_b': jnp.zeros((E,), dtype=jnp.float32), 'w1': jax.random.normal(ks[2], (E, H, F), dtype=jnp.float32) * sc, 'b1': jnp.zeros((E, F), dtype=jnp.float32), 'w2': jax.random.normal(ks[3], (E, F, H), dtype=jnp.float32) * sc, 'b2': jnp.zeros((E, H), dtype=jnp.float32), 'gamma': jnp.ones((H,), dtype=jnp.float32), 'beta': jnp.zeros((H,), dtype=jnp.float32)}
    _L0_ffn_all = _L0_ffn_setup()
    _L0_ffn_in = {k: v for k, v in _L0_ffn_all.items() if k in ('gate_w', 'gate_b', 'w1', 'b1', 'w2', 'b2', 'gamma', 'beta')}
    del _L0_ffn_all
    return {'x': x, 'adj': adj, 'L0_gnn_e_weight': _L0_gnn_in['e_weight'], 'L0_gnn_Wx': _L0_gnn_in['Wx'], 'L0_gnn_Wh': _L0_gnn_in['Wh'], 'L0_gnn_b': _L0_gnn_in['b'], 'L0_ffn_gate_w': _L0_ffn_in['gate_w'], 'L0_ffn_gate_b': _L0_ffn_in['gate_b'], 'L0_ffn_w1': _L0_ffn_in['w1'], 'L0_ffn_b1': _L0_ffn_in['b1'], 'L0_ffn_w2': _L0_ffn_in['w2'], 'L0_ffn_b2': _L0_ffn_in['b2'], 'L0_ffn_gamma': _L0_ffn_in['gamma'], 'L0_ffn_beta': _L0_ffn_in['beta']}

def reference(x, adj, L0_gnn_e_weight, L0_gnn_Wx, L0_gnn_Wh, L0_gnn_b, L0_ffn_gate_w, L0_ffn_gate_b, L0_ffn_w1, L0_ffn_b1, L0_ffn_w2, L0_ffn_b2, L0_ffn_gamma, L0_ffn_beta):
    import jax
    import jax.numpy as jnp

    def _L0_gnn_ref(seq_data, graph, e_weight, Wx, Wh, b):
        import jax, jax.numpy as jnp
        import numpy as np
        EPS = 1e-07
        beta = jnp.einsum('bld,du->blu', seq_data, e_weight)
        norm = jnp.maximum(jnp.sum(graph, axis=2), EPS)
        beta = beta / norm[:, :, None]
        agg = jnp.einsum('blu,blm->bmu', beta, graph)
        B, L, U = agg.shape
        h0 = jnp.zeros((B, U), dtype=agg.dtype)

        def step(h, x):
            h = jnp.tanh(x @ Wx + h @ Wh + b)
            return (h, h)
        _, ys = jax.lax.scan(step, h0, jnp.swapaxes(agg, 0, 1))
        return jnp.swapaxes(ys, 0, 1)

    def _L0_ffn_ref(x, gate_w, gate_b, w1, b1, w2, b2, gamma, beta):
        import jax, jax.numpy as jnp
        import numpy as np
        B, S, H, F, E, K = (8, 2048, 128, 256, 16, 2)
        EPS = 1e-05
        gate_logits = x @ gate_w + gate_b
        topk_vals, topk_idx = jax.lax.top_k(gate_logits, K)
        topk_w = jax.nn.softmax(topk_vals, axis=-1)
        h = jax.nn.relu(jnp.einsum('bsh,ehf->bsef', x, w1) + b1)
        expert_out = jnp.einsum('bsef,efh->bseh', h, w2) + b2
        sel = jnp.take_along_axis(expert_out, topk_idx[:, :, :, None], axis=2)
        moe = jnp.sum(topk_w[..., None] * sel, axis=2)
        y = x + moe
        mu = jnp.mean(y, axis=-1, keepdims=True)
        var = jnp.var(y, axis=-1, keepdims=True)
        return (y - mu) / jnp.sqrt(var + EPS) * gamma + beta
    x = x + _L0_gnn_ref(_layernorm(x, axis=-1), adj, L0_gnn_e_weight, L0_gnn_Wx, L0_gnn_Wh, L0_gnn_b)
    x = x + _L0_ffn_ref(_layernorm(x, axis=-1), L0_ffn_gate_w, L0_ffn_gate_b, L0_ffn_w1, L0_ffn_b1, L0_ffn_w2, L0_ffn_b2, L0_ffn_gamma, L0_ffn_beta)
    return x

_drawn_inputs = setup_inputs


def setup_inputs(seed=0):
    import zlib

    import numpy as np

    out = dict(_drawn_inputs(seed))
    spreads = {'L0_gnn_b': (0.0, 0.1),
     'L0_ffn_gate_b': (0.0, 0.1),
     'L0_ffn_b1': (0.0, 0.8),
     'L0_ffn_b2': (0.0, 0.267),
     'L0_ffn_gamma': (1.0, 0.2),
     'L0_ffn_beta': (0.0, 0.1)}
    factors = {'L0_ffn_w1': 3.836, 'L0_ffn_w2': 3.031}
    for name, (base, spread) in spreads.items():
        noise = np.random.default_rng([zlib.crc32(name.encode()), seed]).standard_normal(out[name].shape)
        drawn = base * np.exp(spread * noise) if base else spread * noise
        out[name] = jnp.asarray(drawn.astype(out[name].dtype))
    for name, factor in factors.items():
        out[name] = (out[name] * factor).astype(out[name].dtype)
    return out
```

```python
from contextlib import ExitStack

import concourse.bass as bass
from concourse import mybir

F32 = mybir.dt.float32
BF16 = mybir.dt.bfloat16
I32 = mybir.dt.int32
U32 = mybir.dt.uint32
ALU = mybir.AluOpType
ACT = mybir.ActivationFunctionType
AX_X = mybir.AxisListType.X

P = 128
GROUPS = 2
NB = P // GROUPS
QUAD = 4
NQ = NB // QUAD
SPQ = 8
UN = 4
GNN_EPS = 1e-7
LN_EPS = 1e-5


def build(nc, x, adj, eW, Wx, Wh, b, gate_w, gate_b, w1, b1, w2, b2, gamma, beta, out):
    NE, _, F = w1.shape
    with ExitStack() as ctx:
        def sb(name, shape, dt=F32):
            return ctx.enter_context(nc.sbuf_tensor(name, shape, dt))

        def sem(name):
            return ctx.enter_context(nc.semaphore(name))

        bank = [ctx.enter_context(nc.psum_tensor(f"bank{i}", [P, 512], F32)) for i in range(8)]
        ps_agg = bank[0:2]
        ps_rnn = bank[2:4]
        ps_ht, ps_xt, ps_lg = bank[4], bank[5], bank[6]

        ident = sb("ident", [P, P])
        center = sb("center", [P, P])
        eW_sb = sb("eW_sb", [P, P])
        Wx_sb = sb("Wx_sb", [P, P])
        Wh_sb = sb("Wh_sb", [P, P])
        bcol = sb("bcol", [P, 1])
        gw_sb = sb("gw_sb", [P, NE])
        gb_bc = sb("gb_bc", [P, NE])
        eWcT = sb("eWcT", [P, P])
        Ec = sb("Ec", [P, P])
        gwc = sb("gwc", [P, NE])
        mhalf = sb("mhalf", [P, QUAD])
        eps_ln = sb("eps_ln", [P, QUAD])
        xq = sb("xq", [P, UN, QUAD * P])
        aq = sb("aq", [P, UN, QUAD * P])
        xs = sb("xs", [P, 2, QUAD * P])
        AX = sb("AX", [P, GROUPS * P, NB])
        HT = sb("HT", [P, 2, QUAD * P])
        x2r = sb("x2r", [P, UN, QUAD * P])
        x1s = sb("x1s", [P, 2, QUAD * P])
        x1T = sb("x1T", [P, 2, QUAD * P])
        R0 = sb("R0", [P, P, P])
        bnb = sb("bnb", [P, 2, QUAD, 6])
        mv = sb("mv", [P, 2, QUAD, 2])
        nrm = sb("nrm", [P, 2, QUAD])
        sc = sb("sc", [P, 5, QUAD])
        bnb2 = sb("bnb2", [P, 2, QUAD, 6])
        mv2 = sb("mv2", [P, P, 2])
        rs2 = sb("rs2", [P, P])
        ve2 = sb("ve2", [P, 2, QUAD])
        lgs = sb("lgs", [P, 2, QUAD, NE])
        mvs = sb("mvs", [P, 2, QUAD, 2])
        mx8 = sb("mx8", [P, 2, QUAD, 8])
        ix8 = sb("ix8", [P, 2, QUAD, 8], U32)
        top_v = sb("top_v", [P, P, 2])
        top_i = sb("top_i", [P, P, 2])

        s_ld = [sem(f"s_ld{i}") for i in range(UN)]
        s_x2 = [sem(f"s_x2{i}") for i in range(UN)]
        s_w = sem("s_w")
        s_const = sem("s_const")
        s_prep = sem("s_prep")
        s_prepe = sem("s_prepe")
        s_bn = sem("s_bn")
        s_st = sem("s_st")
        s_pc = sem("s_pc")
        s_xs = sem("s_xs")
        s_m1 = sem("s_m1")
        s_ae = sem("s_ae")
        s_rn = sem("s_rn")
        s_th = sem("s_th")
        s_ht = sem("s_ht")
        s_x1 = sem("s_x1")
        s_b2 = sem("s_b2")
        s_v2 = sem("s_v2")
        s_pr = sem("s_pr")
        s_r2 = sem("s_r2")
        s_keep = sem("s_keep")
        s_xt = sem("s_xt")
        s_xe = sem("s_xe")
        s_lg = sem("s_lg")
        s_l1 = sem("s_l1")
        s_l2 = sem("s_l2")
        s_mx = sem("s_mx")
        s_ix = sem("s_ix")
        s_kt = sem("s_kt")

        x_bt = x.rearrange("b l d -> l b d")
        a_bt = adj.rearrange("b l m -> l b m")
        x_tb = x.rearrange("(g b) (i two) d -> two g b i d", g=GROUPS, two=2)
        o_tb = out.rearrange("(g b) (i two) d -> two g b i d", g=GROUPS, two=2)

        front = ExitStack()
        block = front.enter_context(nc.Block())

        def hold(eng, semaphore, value):
            eng.wait_ge(s_const, 1)
            eng.wait_ge(semaphore, value)

        def loop(eng, first, last, body):
            body(first)
            if last - first > 1:
                with eng.Fori(first + 1, last) as J:
                    body(J)

        @block.sync
        def _(sp):
            for dst, src in ((eW_sb[:, :], eW), (Wx_sb[:, :], Wx), (Wh_sb[:, :], Wh),
                             (gw_sb[:, :], gate_w), (bcol[:, :], b.rearrange("(u o) -> u o", o=1)),
                             (gb_bc[:, :], gate_b.rearrange("(o e) -> o e", o=1).broadcast_to([P, NE]))):
                sp.dma_start(dst, src).then_inc(s_w, 16)

            def quad(J, u, Q):
                if not (isinstance(Q, int) and Q < UN):
                    sp.wait_ge(s_m1, Q - UN + 1)
                xv = xq[:, u, :].rearrange("p (b d) -> p b d", b=QUAD)
                av = aq[:, u, :].rearrange("p (b d) -> p b d", b=QUAD)
                sp.dma_start(xv, x_bt[:, bass.ds(QUAD * Q, QUAD), :]).then_inc(s_ld[u], 16)
                sp.dma_start(av, a_bt[:, bass.ds(QUAD * Q, QUAD), :]).then_inc(s_ld[u], 16)

            def tiles(u, TQ, g, q):
                if not (isinstance(TQ, int) and TQ < UN):
                    sp.wait_ge(s_x1, TQ - UN + 1)
                for tp in range(2):
                    dst = x2r[tp * NB:(tp + 1) * NB, u, :].rearrange("p (i d) -> p i d", i=QUAD)
                    sp.dma_start(dst, x_tb[tp, g, :, bass.ds(QUAD * q, QUAD), :]).then_inc(s_x2[u], 16)

            def b1(J):
                for u in range(UN):
                    quad(J, u, UN * J + u)
            loop(sp, 0, NQ // UN, b1)

            def b2(J):
                for u in range(UN):
                    quad(J, u, NQ + UN * J + u)
                    tiles(u, UN * J + u, 0, UN * J + u)
            loop(sp, 0, NQ // UN, b2)

            def b3(J):
                for u in range(UN):
                    tiles(u, NQ + UN * J + u, 1, UN * J + u)
            loop(sp, 0, NQ // UN, b3)

        @block.gpsimd
        def _(pool):
            g = nc.gpsimd
            g.memset(ident[:, :], 0.0).then_inc(s_pc, 1)
            g.memset(mhalf[:, :], -0.5)
            g.memset(eps_ln[:, :], LN_EPS)
            pool.wait_ge(s_pc, 1)
            g.affine_select(out=ident[:, :], in_=ident[:, :], compare_op=ALU.not_equal, fill=1.0, base=0,
                            pattern=[[-1, P]], channel_multiplier=1).then_inc(s_pc, 1)
            pool.wait_ge(s_pc, 2)
            g.tensor_scalar(center[:, :], ident[:, :], -1.0 / P, None, ALU.add).then_inc(s_const, 1)

            def scale(u, Q):
                c = 2 + 4 * Q
                pool.wait_ge(s_st, Q + 1)
                h = u % 2
                g.tensor_tensor(sc[:, 1, :], mv[:, h, :, 1], eps_ln[:, :], ALU.add)
                g.tensor_scalar(sc[:, 0, :], nrm[:, h, :], GNN_EPS, None, ALU.max).then_inc(s_pc, 1)
                pool.wait_ge(s_pc, c + 1)
                g.tensor_tensor(sc[:, 2, :], sc[:, 0, :], sc[:, 1, :], ALU.mult).then_inc(s_pc, 1)
                pool.wait_ge(s_pc, c + 2)
                g.tensor_tensor(sc[:, 3, :], sc[:, 0, :], sc[:, 2, :], ALU.mult).then_inc(s_pc, 1)
                pool.wait_ge(s_pc, c + 3)
                g.tensor_tensor(sc[:, 4, :], sc[:, 3, :], mhalf[:, :], ALU.pow).then_inc(s_pc, 1)
                pool.wait_ge(s_pc, c + 4)
                if not (isinstance(Q, int) and Q < 2):
                    pool.wait_ge(s_m1, Q - 1)
                g.tensor_tensor(xs[:, h, :].rearrange("p (b d) -> p b d", b=QUAD),
                                xq[:, u, :].rearrange("p (b d) -> p b d", b=QUAD),
                                sc[:, 4, :].rearrange("p (b o) -> p b o", o=1).broadcast_to([P, QUAD, P]),
                                ALU.mult).then_inc(s_xs, 1)

            def keep(h, TQ):
                pool.wait_ge(s_x1, TQ + 1)
                g.tensor_copy(R0[:, bass.ds(QUAD * TQ, QUAD), :],
                              x1s[:, h, :].rearrange("p (i d) -> p i d", i=QUAD)).then_inc(s_keep, 1)
                pool.wait_ge(s_v2, TQ + 1)
                g.tensor_copy(mv2[:, bass.ds(QUAD * TQ, QUAD), :], mvs[:, h, :, :])
                g.tensor_tensor(ve2[:, h, :], mvs[:, h, :, 1], eps_ln[:, :], ALU.add).then_inc(s_pr, 1)
                pool.wait_ge(s_pr, TQ + 1)
                g.tensor_tensor(rs2[:, bass.ds(QUAD * TQ, QUAD)], ve2[:, h, :], mhalf[:, :],
                                ALU.pow).then_inc(s_r2, 1)
                pool.wait_ge(s_ix, TQ + 1)
                g.tensor_copy(top_v[:, bass.ds(QUAD * TQ, QUAD), :], mx8[:, h, :, 0:2])
                g.tensor_copy(top_i[:, bass.ds(QUAD * TQ, QUAD), :], ix8[:, h, :, 0:2]).then_inc(s_kt, 1)

            def b1(J):
                for u in range(UN):
                    scale(u, UN * J + u)
            loop(pool, 0, NQ // UN, b1)

            def b2(J):
                for u in range(UN):
                    if not (isinstance(J, int) and J == 0 and u == 0):
                        keep((u + 1) % 2, UN * J + u - 1)
                    scale(u, NQ + UN * J + u)
            loop(pool, 0, NQ // UN, b2)

            def b3(J):
                for u in range(UN):
                    keep((u + 1) % 2, NQ + UN * J + u - 1)
            loop(pool, 0, NQ // UN, b3)
            keep(1, 2 * NQ - 1)

        @block.tensor
        def _(pe):
            mm = nc.tensor.matmul
            pe.wait_ge(s_w, 16 * 6)
            pe.wait_ge(s_const, 1)
            mm(bank[7][:, 0:P], eW_sb[:, :], center[:, :], start=True, stop=True).then_inc(s_prep, 1)
            pe.wait_ge(s_prepe, 1)
            mm(bank[7][:, P:2 * P], eWcT[:, :], Wx_sb[:, :], start=True, stop=True)
            mm(bank[7][:, 2 * P:2 * P + NE], center[:, :], gw_sb[:, :], start=True, stop=True).then_inc(s_prep, 1)
            pe.wait_ge(s_prepe, 2)

            def agg(u, Q, j):
                if j == 0:
                    pe.wait_ge(s_xs, Q + 1)
                    if not (isinstance(Q, int) and Q < 2):
                        pe.wait_ge(s_ae, Q - 1)
                i = mm(ps_agg[u % 2][:, j * P:(j + 1) * P], xs[:, u % 2, j * P:(j + 1) * P],
                       aq[:, u, j * P:(j + 1) * P], start=True, stop=True)
                if j == QUAD - 1:
                    i.then_inc(s_m1, 1)

            def turn_h(h, TQ):
                pe.wait_ge(s_th, SPQ * TQ + SPQ)
                if not (isinstance(TQ, int) and TQ < 1):
                    pe.wait_ge(s_x1, TQ)
                for j in range(QUAD):
                    i = nc.tensor.transpose(ps_ht[:, j * P:(j + 1) * P], HT[:, h, j * P:(j + 1) * P], ident[:, :])
                i.then_inc(s_ht, 1)

            def turn_x(h, TQ):
                pe.wait_ge(s_x1, TQ + 1)
                if not (isinstance(TQ, int) and TQ < 1):
                    pe.wait_ge(s_xe, TQ)
                for j in range(QUAD):
                    i = nc.tensor.transpose(ps_xt[:, j * P:(j + 1) * P], x1s[:, h, j * P:(j + 1) * P], ident[:, :])
                i.then_inc(s_xt, 1)

            def logits(h, TQ):
                pe.wait_ge(s_xe, TQ + 1)
                if not (isinstance(TQ, int) and TQ < 1):
                    pe.wait_ge(s_l1, TQ)
                for j in range(QUAD):
                    i = mm(ps_lg[:, j * NE:(j + 1) * NE], x1T[:, h, j * P:(j + 1) * P], gwc[:, :],
                           start=True, stop=True)
                i.then_inc(s_lg, 1)

            def steps(RQ, fresh, h_tile, TQ, agg_u, aggQ):
                for k in range(SPQ):
                    S = SPQ * RQ + k
                    first = fresh and k == 0
                    if not (isinstance(S, int) and S < 2):
                        pe.wait_ge(s_th, S - 1)
                    o = ps_rnn[k % 2][:, 0:NB]
                    i = mm(o, Ec[:, :], AX[:, S, :], start=True, stop=first)
                    if first:
                        i.then_inc(s_rn, 1)
                    if TQ is not None:
                        if k == 1:
                            turn_h(h_tile, TQ)
                        if k == 4:
                            turn_x(h_tile, TQ)
                        if k == 7:
                            logits(h_tile, TQ)
                    if agg_u is not None and 2 <= k < 2 + QUAD:
                        agg(agg_u, aggQ, k - 2)
                    if not first:
                        pe.wait_ge(s_th, S)
                        prev = HT[:, (u_of[0] + (0 if k else 1)) % 2, ((k - 1) % SPQ) * NB:((k - 1) % SPQ + 1) * NB]
                        mm(o, Wh_sb[:, :], prev, start=False, stop=True).then_inc(s_rn, 1)

            u_of = [0]

            def b1(J):
                for u in range(UN):
                    for j in range(QUAD):
                        agg(u, UN * J + u, j)
            loop(pe, 0, NQ // UN, b1)
            pe.wait_ge(s_ae, NQ)

            def b2(J):
                for u in range(UN):
                    u_of[0] = u
                    start = isinstance(J, int) and J == 0 and u == 0
                    steps(UN * J + u, start, (u + 1) % 2, None if start else UN * J + u - 1,
                          None if start else (u - 1) % UN, NQ + UN * J + u - 1)
            loop(pe, 0, NQ // UN, b2)
            for j in range(QUAD):
                agg(UN - 1, 2 * NQ - 1, j)
            pe.wait_ge(s_ae, 2 * NQ)

            def b3(J):
                for u in range(UN):
                    u_of[0] = u
                    steps(NQ + UN * J + u, isinstance(J, int) and J == 0 and u == 0, (u + 1) % 2,
                          NQ + UN * J + u - 1, None, None)
            loop(pe, 0, NQ // UN, b3)
            turn_h(1, 2 * NQ - 1)
            turn_x(1, 2 * NQ - 1)
            logits(1, 2 * NQ - 1)

        @block.scalar
        def _(act):
            a = nc.scalar.activation
            act.wait_ge(s_prep, 1)
            nc.scalar.copy(eWcT[:, :], bank[7][:, 0:P]).then_inc(s_prepe, 1)
            act.wait_ge(s_prep, 2)
            nc.scalar.copy(Ec[:, :], bank[7][:, P:2 * P])
            nc.scalar.copy(gwc[:, :], bank[7][:, 2 * P:2 * P + NE]).then_inc(s_prepe, 1)

            def agg_out(u, Q, g, q):
                act.wait_ge(s_m1, Q + 1)
                nc.scalar.copy(AX[:, g * P:(g + 1) * P, bass.ds(QUAD * q, QUAD)],
                               ps_agg[u % 2][:, :].rearrange("p (b t) -> p t b", b=QUAD)).then_inc(s_ae, 1)

            def x1T_out(h, TQ):
                act.wait_ge(s_xt, TQ + 1)
                if not (isinstance(TQ, int) and TQ < 2):
                    act.wait_ge(s_lg, TQ - 1)
                nc.scalar.copy(x1T[:, h, :], ps_xt[:, :]).then_inc(s_xe, 1)

            def steps(u, RQ, TQ, aggu, aggQ, aggq):
                for k in range(SPQ):
                    S = SPQ * RQ + k
                    if k == 0 and not (isinstance(RQ, int) and RQ < 2):
                        act.wait_ge(s_ht, RQ - 1)
                    act.wait_ge(s_rn, S + 1)
                    a(HT[:, u % 2, k * NB:(k + 1) * NB], ps_rnn[k % 2][:, 0:NB], ACT.Tanh,
                      bias=bcol[:, :]).then_inc(s_th, 1)
                    if k == 5 and TQ is not None:
                        x1T_out((u + 1) % 2, TQ)
                    if k == 6 and aggu is not None:
                        agg_out(aggu, aggQ, 1, aggq)

            def b1(J):
                for u in range(UN):
                    agg_out(u, UN * J + u, 0, UN * J + u)
            loop(act, 0, NQ // UN, b1)

            def b2(J):
                for u in range(UN):
                    start = isinstance(J, int) and J == 0 and u == 0
                    q = UN * J + u - 1
                    steps(u, UN * J + u, None if start else q, None if start else (u - 1) % UN, NQ + q, q)
            loop(act, 0, NQ // UN, b2)
            agg_out(UN - 1, 2 * NQ - 1, 1, NQ - 1)

            def b3(J):
                for u in range(UN):
                    steps(u, NQ + UN * J + u, NQ + UN * J + u - 1, None, None, None)
            loop(act, 0, NQ // UN, b3)
            x1T_out(1, 2 * NQ - 1)

        @block.vector
        def _(dve):
            v = nc.vector

            def stats(u, Q):
                n = Q + 1
                h = u % 2
                dve.wait_ge(s_ld[u], (Q - u) * 8 + 32)
                if not (isinstance(Q, int) and Q < 2):
                    dve.wait_ge(s_xs, Q - 1)
                for j in range(QUAD):
                    i = v.bn_stats(bnb[:, h, j, :], xq[:, u, j * P:(j + 1) * P])
                i.then_inc(s_bn, 1)
                dve.wait_ge(s_bn, n)
                v.tensor_reduce(nrm[:, h, :], aq[:, u, :].rearrange("p (b d) -> p b d", b=QUAD), AX_X, ALU.add)
                for j in range(QUAD):
                    i = v.bn_aggr(mv[:, h, j, :], bnb[:, h, j, :])
                i.then_inc(s_st, 1)

            def tile_a(u, h, TQ):
                dve.wait_ge(s_ht, TQ + 1)
                dve.wait_ge(s_x2[u], (TQ - u) * 8 + 32)
                if not (isinstance(TQ, int) and TQ < 2):
                    dve.wait_ge(s_keep, TQ - 1)
                    dve.wait_ge(s_xt, TQ - 1)
                v.tensor_tensor(x1s[:, h, :], ps_ht[:, :], x2r[:, u, :], ALU.add).then_inc(s_x1, 1)

            def tile_b(u, h, TQ):
                dve.wait_ge(s_x1, TQ + 1)
                for j in range(QUAD):
                    i = v.bn_stats(bnb2[:, h, j, :], x1s[:, h, j * P:(j + 1) * P])
                i.then_inc(s_b2, 1)
                hold(dve, s_b2, TQ + 1)
                if not (isinstance(TQ, int) and TQ < 2):
                    dve.wait_ge(s_r2, TQ - 1)
                for j in range(QUAD):
                    i = v.bn_aggr(mvs[:, h, j, :], bnb2[:, h, j, :])
                i.then_inc(s_v2, 1)

            def tile_c(u, h, TQ):
                dve.wait_ge(s_lg, TQ + 1)
                dve.wait_ge(s_r2, TQ + 1)
                v.tensor_tensor(lgs[:, h, :, :], ps_lg[:, 0:QUAD * NE].rearrange("p (i e) -> p i e", i=QUAD),
                                rs2[:, bass.ds(QUAD * TQ, QUAD)].rearrange("p (i o) -> p i o", o=1)
                                .broadcast_to([P, QUAD, NE]), ALU.mult).then_inc(s_l1, 1)
                dve.wait_ge(s_l1, TQ + 1)
                v.tensor_tensor(lgs[:, h, :, :], lgs[:, h, :, :],
                                gb_bc[:, :].rearrange("p (o e) -> p o e", o=1).broadcast_to([P, QUAD, NE]),
                                ALU.add).then_inc(s_l2, 1)
                hold(dve, s_l2, TQ + 1)
                if not (isinstance(TQ, int) and TQ < 2):
                    dve.wait_ge(s_kt, TQ - 1)
                for j in range(QUAD):
                    i = v.max(mx8[:, h, j, :], lgs[:, h, j, :])
                i.then_inc(s_mx, 1)
                hold(dve, s_mx, TQ + 1)
                for j in range(QUAD):
                    i = v.max_index(ix8[:, h, j, :], mx8[:, h, j, :], lgs[:, h, j, :])
                i.then_inc(s_ix, 1)

            def b1(J):
                for u in range(UN):
                    stats(u, UN * J + u)
            loop(dve, 0, NQ // UN, b1)
            dve.wait_ge(s_w, 16 * 6)

            def b2(J):
                for u in range(UN):
                    t = (u - 1) % UN, (u + 1) % 2, UN * J + u - 1
                    start = isinstance(J, int) and J == 0 and u == 0
                    if not start:
                        tile_a(*t)
                        tile_b(*t)
                    stats(u, NQ + UN * J + u)
                    if not start:
                        tile_c(*t)
            loop(dve, 0, NQ // UN, b2)

            def b3(J):
                for u in range(UN):
                    t = (u - 1) % UN, (u + 1) % 2, NQ + UN * J + u - 1
                    tile_a(*t)
                    tile_b(*t)
                    tile_c(*t)
            loop(dve, 0, NQ // UN, b3)
            t = UN - 1, 1, 2 * NQ - 1
            tile_a(*t)
            tile_b(*t)
            tile_c(*t)

        front.close()

        W1 = AX[:, 80:144, :].rearrange("p a b -> p (a b)").rearrange("p (e f) -> p e f", e=NE)
        W2 = AX[:, 144:208, :].rearrange("p a b -> p (a b)").rearrange("p (e c f) -> p e c f", e=NE, c=2)
        b1c = sb("b1c", [P, NE, 2])
        b2r = sb("b2r", [1, NE * P])
        ones = sb("ones", [1, P])
        gm_bc = sb("gm_bc", [P, P])
        bt_bc = sb("bt_bc", [P, P])
        Gt = AX[:, 0:32, :].rearrange("p a b -> p (a b)").rearrange("p (t e) -> p t e", e=NE)
        Gu = AX[:, 32:64, :].rearrange("p a b -> p (a b)").rearrange("p (t e) -> p t e", e=NE)
        ixf = AX[:, 64:80, :].rearrange("p a b -> p (a b)").rearrange("p (t e) -> p t e", e=8)
        e2 = sb("e2", [P, P])
        w_1 = sb("w_1", [P, P])
        w_2 = sb("w_2", [P, P])
        zs = sb("zs", [P, 512])
        zT = sb("zT", [P, 512])
        acc = sb("acc", [P, 512])
        hs = sb("hs", [P, 2, 512])
        nmr = sb("nmr", [P, P])
        fst = sb("fst", [P, QUAD, 6])
        fmv = sb("fmv", [P, QUAD, 2])
        frs = sb("frs", [P, QUAD])
        iota_e = sb("iota_e", [P, NE])
        d = {k: sem("d_" + k) for k in ("w", "c", "v", "e", "z", "zt", "ze", "h", "hr", "o", "acc", "b", "r", "out", "p")}

        with nc.Block() as block:
            @block.sync
            def _(sp):
                sp.dma_start(W1, w1.rearrange("e h f -> h e f")).then_inc(d["w"], 16)
                sp.dma_start(W2, w2.rearrange("e (c f) h -> f e c h", c=2)).then_inc(d["w"], 16)
                for c in range(2):
                    sp.dma_start(b1c[:, :, c], b1.rearrange("e (c f) -> c f e", c=2)[c], allow_slow_non_contiguous=True).then_inc(d["w"], 16)
                sp.dma_start(b2r[:, :], b2.rearrange("(o e) h -> o (e h)", o=1)).then_inc(d["w"], 16)
                sp.dma_start(gm_bc[:, :], gamma.rearrange("(o e) -> o e", o=1).broadcast_to([P, P])).then_inc(d["w"], 16)
                sp.dma_start(bt_bc[:, :], beta.rearrange("(o e) -> o e", o=1).broadcast_to([P, P])).then_inc(d["w"], 16)
                for g in range(2):
                    with sp.Fori(0, NQ) as q:
                        TQ = q + NQ * g
                        sp.wait_ge(d["b"], 4 * TQ + 4)
                        for tp in range(2):
                            sp.dma_start(o_tb[tp, g, :, bass.ds(QUAD * q, QUAD), :],
                                         acc[tp * NB:(tp + 1) * NB, :].rearrange("p (i d) -> p i d", i=QUAD)).then_inc(d["out"], 16)
                sp.wait_ge(d["out"], 32 * 32)

            @block.gpsimd
            def _(pool):
                nc.gpsimd.memset(ones[:, :], 1.0)
                nc.gpsimd.iota(iota_e[:, :], [[1, NE]], base=0, channel_multiplier=0, allow_small_or_imprecise_dtypes=True).then_inc(d["c"], 1)
                with pool.Fori(0, 32) as TQ:
                    pool.wait_ge(d["r"], TQ + 1)
                    nc.gpsimd.tensor_tensor(frs[:, :], frs[:, :], mhalf[:, :], ALU.pow).then_inc(d["p"], 1)

            @block.tensor
            def _(pe):
                mm = nc.tensor.matmul
                pe.wait_ge(d["w"], 16 * 7)
                pe.wait_ge(d["c"], 1)
                with pe.Fori(0, 32) as TQ:
                    pe.wait_ge(d["z"], TQ + 1)
                    for j in range(QUAD):
                        i = nc.tensor.transpose(ps_ht[:, j * P:(j + 1) * P], zs[:, j * P:(j + 1) * P], ident[:, :])
                    i.then_inc(d["zt"], 1)
                    pe.wait_ge(d["ze"], TQ + 1)
                    for e in range(NE):
                        for c in range(2):
                            mm(ps_rnn[c][:, :], W1[:, e, c * P:(c + 1) * P], zT[:, :], start=True, stop=True).then_inc(d["h"], 1)
                        pe.wait_ge(d["hr"], 2 * NE * TQ + 2 * e + 2)
                        for j in range(QUAD):
                            o = ps_agg[0][:, j * P:(j + 1) * P]
                            mm(o, hs[:, 0, j * P:(j + 1) * P], W2[:, e, 0, :], start=True, stop=False)
                            mm(o, hs[:, 1, j * P:(j + 1) * P], W2[:, e, 1, :], start=False, stop=False)
                            i = mm(o, ones[:, :], b2r[:, e * P:(e + 1) * P], start=False, stop=True)
                        i.then_inc(d["o"], 1)
                        pe.wait_ge(d["acc"], NE * TQ + e + 1)

            @block.scalar
            def _(act):
                act.wait_ge(d["w"], 16 * 7)
                act.wait_ge(d["v"], 1)
                nc.scalar.activation(e2[:, :], e2[:, :], ACT.Exp).then_inc(d["e"], 1)
                with act.Fori(0, 32) as TQ:
                    act.wait_ge(d["zt"], TQ + 1)
                    nc.scalar.copy(zT[:, :], ps_ht[:, :]).then_inc(d["ze"], 1)
                    for e in range(NE):
                        for c in range(2):
                            act.wait_ge(d["h"], 2 * NE * TQ + 2 * e + c + 1)
                            nc.scalar.activation(hs[:, c, :], ps_rnn[c][:, :], ACT.Relu, bias=b1c[:, e, c:c + 1]).then_inc(d["hr"], 1)

            @block.vector
            def _(dve):
                v = nc.vector
                n = [0]
                s_c = sem("d_chain")
                s_f = sem("d_final")

                def link(i):
                    n[0] += 1
                    i.then_inc(s_c, 1)
                    dve.wait_ge(s_c, n[0])
                dve.wait_ge(d["w"], 16 * 7)
                dve.wait_ge(d["c"], 1)
                v.tensor_tensor(e2[:, :], top_v[:, :, 1], top_v[:, :, 0], ALU.subtract).then_inc(d["v"], 1)
                dve.wait_ge(d["e"], 1)
                link(v.tensor_scalar(w_1[:, :], e2[:, :], 1.0, None, ALU.add))
                link(v.reciprocal(w_1[:, :], w_1[:, :]))
                link(v.tensor_tensor(w_2[:, :], w_1[:, :], e2[:, :], ALU.mult))
                

                def bc(t):
                    return t.rearrange("p (t o) -> p t o", o=1).broadcast_to([P, P, NE])
                io = iota_e[:, :].rearrange("p (o e) -> p o e", o=1).broadcast_to([P, P, NE])
                link(v.tensor_tensor(Gt, io, top_i[:, :, 0:1].broadcast_to([P, P, NE]), ALU.is_equal))
                link(v.tensor_tensor(Gt, Gt, bc(w_1[:, :]), ALU.mult))
                link(v.tensor_tensor(Gu, io, top_i[:, :, 1:2].broadcast_to([P, P, NE]), ALU.is_equal))
                link(v.tensor_tensor(Gu, Gu, bc(w_2[:, :]), ALU.mult))
                link(v.tensor_tensor(Gt, Gt, Gu, ALU.add))
                link(v.tensor_tensor(nmr[:, :], mv2[:, :, 0], rs2[:, :], ALU.mult))
                link(v.tensor_scalar(nmr[:, :], nmr[:, :], -1.0, None, ALU.mult))
                with dve.Fori(0, 32) as TQ:
                    if True:
                        for j in range(QUAD):
                            T = QUAD * TQ + j
                            i = v.tensor_scalar(zs[:, j * P:(j + 1) * P], R0[:, T, :], rs2[:, bass.ds(T, 1)], nmr[:, bass.ds(T, 1)], ALU.mult, ALU.add)
                        i.then_inc(d["z"], 1)
                        dve.wait_ge(d["z"], TQ + 1)
                        dve.wait_ge(d["out"], 32 * TQ)
                        v.tensor_copy(acc[:, :], zs[:, :]).then_inc(d["b"], 1)
                        dve.wait_ge(d["b"], 4 * TQ + 1)
                        for e in range(NE):
                            dve.wait_ge(d["o"], NE * TQ + e + 1)
                            if e:
                                dve.wait_ge(d["acc"], NE * TQ + e)
                            for j in range(QUAD):
                                T = QUAD * TQ + j
                                a = acc[:, j * P:(j + 1) * P]
                                i = v.scalar_tensor_tensor(out=a, in0=ps_agg[0][:, j * P:(j + 1) * P], scalar=Gt[:, T, e:e + 1],
                                                           in1=a, op0=ALU.mult, op1=ALU.add)
                            i.then_inc(d["acc"], 1)
                        dve.wait_ge(d["acc"], NE * TQ + NE)
                        for j in range(QUAD):
                            i = v.bn_stats(fst[:, j, :], acc[:, j * P:(j + 1) * P])
                        i.then_inc(d["b"], 1)
                        hold(dve, d["b"], 4 * TQ + 2)
                        for j in range(QUAD):
                            i = v.bn_aggr(fmv[:, j, :], fst[:, j, :])
                        i.then_inc(d["b"], 1)
                        dve.wait_ge(d["b"], 4 * TQ + 3)
                        v.tensor_scalar(frs[:, :], fmv[:, :, 1], LN_EPS, None, ALU.add).then_inc(d["r"], 1)
                        dve.wait_ge(d["p"], TQ + 1)
                        for j in range(QUAD):
                            a = acc[:, j * P:(j + 1) * P]
                            i = v.tensor_scalar(a, a, fmv[:, j, 0:1], frs[:, j:j + 1], ALU.subtract, ALU.mult)
                        i.then_inc(s_f, 1)
                        dve.wait_ge(s_f, 3 * TQ + 1)
                        a4 = acc[:, :].rearrange("p (j d) -> p j d", j=QUAD)

                        def bd(t):
                            return t[:, :].rearrange("p (o d) -> p o d", o=1).broadcast_to([P, QUAD, P])
                        v.tensor_tensor(a4, a4, bd(gm_bc), ALU.mult).then_inc(s_f, 1)
                        dve.wait_ge(s_f, 3 * TQ + 2)
                        v.tensor_tensor(a4, a4, bd(bt_bc), ALU.add).then_inc(s_f, 1)
                        dve.wait_ge(s_f, 3 * TQ + 3)
                        v.tensor_tensor(a4, a4, R0[:, bass.ds(QUAD * TQ, QUAD), :], ALU.add).then_inc(d["b"], 1)


_INS = ['x', 'adj', 'L0_gnn_e_weight', 'L0_gnn_Wx', 'L0_gnn_Wh', 'L0_gnn_b', 'L0_ffn_gate_w', 'L0_ffn_gate_b',
        'L0_ffn_w1', 'L0_ffn_b1', 'L0_ffn_w2', 'L0_ffn_b2', 'L0_ffn_gamma', 'L0_ffn_beta']


def kernel(**inputs):
    import numpy as _np
    import concourse.bacc as _bacc
    from concourse import mybir as _mybir
    from concourse.bass_utils import run_bass_kernel_spmd as _run

    nc = _bacc.Bacc("TRN2", target_bir_lowering=False, num_devices=1)
    arrays, args = {}, []
    for name in _INS:
        a = _np.ascontiguousarray(inputs[name])
        arrays[f"in_{name}_dram"] = a
        args.append(nc.dram_tensor(f"in_{name}_dram", a.shape, _mybir.dt.from_np(a.dtype), kind="ExternalInput").ap())
    args.append(nc.dram_tensor("out_0_dram", inputs['x'].shape, F32, kind="ExternalOutput").ap())
    build(nc, *args)
    r = _run(nc, [arrays], core_ids=[0])
    return r.results[0]["out_0_dram"]
```

```python
from contextlib import ExitStack

import concourse.bass as bass
from concourse import mybir

F32 = mybir.dt.float32
BF16 = mybir.dt.bfloat16
I32 = mybir.dt.int32
U32 = mybir.dt.uint32
ALU = mybir.AluOpType
ACT = mybir.ActivationFunctionType
AX_X = mybir.AxisListType.X

P = 128
GROUPS = 2
NB = P // GROUPS
QUAD = 4
NQ = NB // QUAD
SPQ = 8
UN = 4
GNN_EPS = 1e-7
LN_EPS = 1e-5
C_RSTD, C_NMR, C_W1, C_W2, C_POS2, C_TOKEN = range(P, P + 6)
W_A = P + 6
W_B = W_A + P
NOWHERE = 1 << 16


def build(nc, x, adj, eW, Wx, Wh, b, gate_w, gate_b, w1, b1, w2, b2, gamma, beta, out):
    NE, _, F = w1.shape
    NBLK = P + NE
    NQUAD = NBLK // QUAD
    NIT = NBLK + 8
    with ExitStack() as ctx:
        def sb(name, shape, dt=F32):
            return ctx.enter_context(nc.sbuf_tensor(name, shape, dt))

        front = ExitStack()

        def fsb(name, shape, dt=F32):
            return front.enter_context(nc.sbuf_tensor(name, shape, dt))

        def sem(name):
            return ctx.enter_context(nc.semaphore(name))

        bank = [ctx.enter_context(nc.psum_tensor(f"bank{i}", [P, 512], F32)) for i in range(8)]
        ps_agg = bank[0:2]
        ps_rnn = bank[2:4]
        ps_ht, ps_xt, ps_lg = bank[4], bank[5], bank[6]

        ident = sb("ident", [P, P])
        mhalf = sb("mhalf", [P, QUAD])
        eps_ln = sb("eps_ln", [P, QUAD])
        rows = sb("rows", [P, P, W_A])
        mv2 = sb("mv2", [P, P, 2])
        rs2 = sb("rs2", [P, P])
        top_v = sb("top_v", [P, P, 2])
        top_i = sb("top_i", [P, P, 2])
        filler = sb("filler", [P, W_B])
        center = fsb("center", [P, P])
        eW_sb = fsb("eW_sb", [P, P])
        Wx_sb = fsb("Wx_sb", [P, P])
        Wh_sb = fsb("Wh_sb", [P, P])
        bcol = fsb("bcol", [P, 1])
        gw_sb = fsb("gw_sb", [P, NE])
        gb_bc = fsb("gb_bc", [P, NE])
        eWcT = fsb("eWcT", [P, P])
        Ec = fsb("Ec", [P, P])
        gwc = fsb("gwc", [P, NE])
        xq = fsb("xq", [P, UN, QUAD * P])
        aq = fsb("aq", [P, UN, QUAD * P])
        xs = fsb("xs", [P, 2, QUAD * P])
        AX = fsb("AX", [P, GROUPS * P, NB])
        HT = fsb("HT", [P, 2, QUAD * P])
        x2r = fsb("x2r", [P, UN, QUAD * P])
        x1s = fsb("x1s", [P, 2, QUAD * P])
        x1T = fsb("x1T", [P, 2, QUAD * P])
        bnb = fsb("bnb", [P, 2, QUAD, 6])
        mv = fsb("mv", [P, 2, QUAD, 2])
        nrm = fsb("nrm", [P, 2, QUAD])
        sc = fsb("sc", [P, 5, QUAD])
        bnb2 = fsb("bnb2", [P, 2, QUAD, 6])
        ve2 = fsb("ve2", [P, 2, QUAD])
        lgs = fsb("lgs", [P, 2, QUAD, NE])
        mvs = fsb("mvs", [P, 2, QUAD, 2])
        mx8 = fsb("mx8", [P, 2, QUAD, 8])
        ix8 = fsb("ix8", [P, 2, QUAD, 8], U32)

        s_ld = [sem(f"s_ld{i}") for i in range(UN)]
        s_x2 = [sem(f"s_x2{i}") for i in range(UN)]
        s_w = sem("s_w")
        s_const = sem("s_const")
        s_prep = sem("s_prep")
        s_prepe = sem("s_prepe")
        s_bn = sem("s_bn")
        s_st = sem("s_st")
        s_pc = sem("s_pc")
        s_xs = sem("s_xs")
        s_m1 = sem("s_m1")
        s_ae = sem("s_ae")
        s_rn = sem("s_rn")
        s_th = sem("s_th")
        s_ht = sem("s_ht")
        s_x1 = sem("s_x1")
        s_b2 = sem("s_b2")
        s_v2 = sem("s_v2")
        s_pr = sem("s_pr")
        s_r2 = sem("s_r2")
        s_keep = sem("s_keep")
        s_xt = sem("s_xt")
        s_xe = sem("s_xe")
        s_lg = sem("s_lg")
        s_l1 = sem("s_l1")
        s_l2 = sem("s_l2")
        s_mx = sem("s_mx")
        s_ix = sem("s_ix")
        s_kt = sem("s_kt")
        s_fill = sem("s_fill")
        s_fv = sem("s_fv")

        dram_a = nc.dram_tensor("rows_by_first", [NBLK * P, W_A], F32)
        dram_b = nc.dram_tensor("rows_by_second", [NBLK * P, W_B], F32)

        x_bt = x.rearrange("b l d -> l b d")
        a_bt = adj.rearrange("b l m -> l b m")
        x_tb = x.rearrange("(g b) (i two) d -> two g b i d", g=GROUPS, two=2)
        o_tb = out.rearrange("(g b) (i two) d -> two g b i d", g=GROUPS, two=2)

        block = front.enter_context(nc.Block())

        def hold(eng, semaphore, value):
            value = value if isinstance(value, int) else eng.to_reg(value)
            eng.wait_ge(s_const, 1)
            eng.wait_ge(semaphore, value)

        def loop(eng, first, last, body):
            body(first)
            if last - first > 1:
                with eng.Fori(first + 1, last) as J:
                    body(J)

        @block.sync
        def _(sp):
            for dst, src in ((eW_sb[:, :], eW), (Wx_sb[:, :], Wx), (Wh_sb[:, :], Wh),
                             (gw_sb[:, :], gate_w), (bcol[:, :], b.rearrange("(u o) -> u o", o=1)),
                             (gb_bc[:, :], gate_b.rearrange("(o e) -> o e", o=1).broadcast_to([P, NE]))):
                sp.dma_start(dst, src).then_inc(s_w, 16)

            def quad(J, u, Q):
                if not (isinstance(Q, int) and Q < UN):
                    sp.wait_ge(s_m1, Q - UN + 1)
                xv = xq[:, u, :].rearrange("p (b d) -> p b d", b=QUAD)
                av = aq[:, u, :].rearrange("p (b d) -> p b d", b=QUAD)
                sp.dma_start(xv, x_bt[:, bass.ds(QUAD * Q, QUAD), :]).then_inc(s_ld[u], 16)
                sp.dma_start(av, a_bt[:, bass.ds(QUAD * Q, QUAD), :]).then_inc(s_ld[u], 16)

            def tiles(u, TQ, g, q):
                if not (isinstance(TQ, int) and TQ < UN):
                    sp.wait_ge(s_x1, TQ - UN + 1)
                for tp in range(2):
                    dst = x2r[tp * NB:(tp + 1) * NB, u, :].rearrange("p (i d) -> p i d", i=QUAD)
                    sp.dma_start(dst, x_tb[tp, g, :, bass.ds(QUAD * q, QUAD), :]).then_inc(s_x2[u], 16)

            def b1(J):
                for u in range(UN):
                    quad(J, u, UN * J + u)
            loop(sp, 0, NQ // UN, b1)

            def fill(J):
                n = NBLK // 8
                for dram, w in ((dram_a, W_A), (dram_b, W_B)):
                    sp.dma_start(dram.ap().rearrange("(i p) w -> p i w", p=P)[:, bass.ds(n * J, n), :],
                                 filler[:, 0:w].rearrange("p (o w) -> p o w", o=1).broadcast_to([P, n, w])
                                 ).then_inc(s_fill, 16)

            def b2(J):
                for u in range(UN):
                    quad(J, u, NQ + UN * J + u)
                    tiles(u, UN * J + u, 0, UN * J + u)
                if isinstance(J, int):
                    sp.wait_ge(s_fv, 1)
                fill(J)
            loop(sp, 0, NQ // UN, b2)

            def b3(J):
                for u in range(UN):
                    tiles(u, NQ + UN * J + u, 1, UN * J + u)
                fill(J + 4)
            loop(sp, 0, NQ // UN, b3)

        @block.gpsimd
        def _(pool):
            g = nc.gpsimd
            g.memset(ident[:, :], 0.0).then_inc(s_pc, 1)
            g.memset(mhalf[:, :], -0.5)
            g.memset(eps_ln[:, :], LN_EPS)
            pool.wait_ge(s_pc, 1)
            g.affine_select(out=ident[:, :], in_=ident[:, :], compare_op=ALU.not_equal, fill=1.0, base=0,
                            pattern=[[-1, P]], channel_multiplier=1).then_inc(s_pc, 1)
            pool.wait_ge(s_pc, 2)
            g.tensor_scalar(center[:, :], ident[:, :], -1.0 / P, None, ALU.add).then_inc(s_const, 1)

            g.memset(filler[:, :], 0.0).then_inc(s_pc, 1)
            pool.wait_ge(s_pc, 3)
            g.iota(filler[:, C_POS2:C_TOKEN + 1].bitcast(I32), [[0, 2]], base=NOWHERE,
                   channel_multiplier=1).then_inc(s_fv, 1)

            def scale(u, Q):
                c = 3 + 4 * Q
                pool.wait_ge(s_st, Q + 1)
                h = u % 2
                g.tensor_tensor(sc[:, 1, :], mv[:, h, :, 1], eps_ln[:, :], ALU.add)
                g.tensor_scalar(sc[:, 0, :], nrm[:, h, :], GNN_EPS, None, ALU.max).then_inc(s_pc, 1)
                pool.wait_ge(s_pc, c + 1)
                g.tensor_tensor(sc[:, 2, :], sc[:, 0, :], sc[:, 1, :], ALU.mult).then_inc(s_pc, 1)
                pool.wait_ge(s_pc, c + 2)
                g.tensor_tensor(sc[:, 3, :], sc[:, 0, :], sc[:, 2, :], ALU.mult).then_inc(s_pc, 1)
                pool.wait_ge(s_pc, c + 3)
                g.tensor_tensor(sc[:, 4, :], sc[:, 3, :], mhalf[:, :], ALU.pow).then_inc(s_pc, 1)
                pool.wait_ge(s_pc, c + 4)
                if not (isinstance(Q, int) and Q < 2):
                    pool.wait_ge(s_m1, Q - 1)
                g.tensor_tensor(xs[:, h, :].rearrange("p (b d) -> p b d", b=QUAD),
                                xq[:, u, :].rearrange("p (b d) -> p b d", b=QUAD),
                                sc[:, 4, :].rearrange("p (b o) -> p b o", o=1).broadcast_to([P, QUAD, P]),
                                ALU.mult).then_inc(s_xs, 1)

            def keep(h, TQ):
                pool.wait_ge(s_x1, TQ + 1)
                g.tensor_copy(rows[:, bass.ds(QUAD * TQ, QUAD), 0:P],
                              x1s[:, h, :].rearrange("p (i d) -> p i d", i=QUAD)).then_inc(s_keep, 1)
                pool.wait_ge(s_v2, TQ + 1)
                g.tensor_copy(mv2[:, bass.ds(QUAD * TQ, QUAD), :], mvs[:, h, :, :])
                g.tensor_tensor(ve2[:, h, :], mvs[:, h, :, 1], eps_ln[:, :], ALU.add).then_inc(s_pr, 1)
                pool.wait_ge(s_pr, TQ + 1)
                g.tensor_tensor(rs2[:, bass.ds(QUAD * TQ, QUAD)], ve2[:, h, :], mhalf[:, :],
                                ALU.pow).then_inc(s_r2, 1)
                pool.wait_ge(s_ix, TQ + 1)
                g.tensor_copy(top_v[:, bass.ds(QUAD * TQ, QUAD), :], mx8[:, h, :, 0:2])
                g.tensor_copy(top_i[:, bass.ds(QUAD * TQ, QUAD), :], ix8[:, h, :, 0:2]).then_inc(s_kt, 1)

            def b1(J):
                for u in range(UN):
                    scale(u, UN * J + u)
            loop(pool, 0, NQ // UN, b1)

            def b2(J):
                for u in range(UN):
                    if not (isinstance(J, int) and J == 0 and u == 0):
                        keep((u + 1) % 2, UN * J + u - 1)
                    scale(u, NQ + UN * J + u)
            loop(pool, 0, NQ // UN, b2)

            def b3(J):
                for u in range(UN):
                    keep((u + 1) % 2, NQ + UN * J + u - 1)
            loop(pool, 0, NQ // UN, b3)
            keep(1, 2 * NQ - 1)

        @block.tensor
        def _(pe):
            mm = nc.tensor.matmul
            pe.wait_ge(s_w, 16 * 6)
            pe.wait_ge(s_const, 1)
            mm(bank[7][:, 0:P], eW_sb[:, :], center[:, :], start=True, stop=True).then_inc(s_prep, 1)
            pe.wait_ge(s_prepe, 1)
            mm(bank[7][:, P:2 * P], eWcT[:, :], Wx_sb[:, :], start=True, stop=True)
            mm(bank[7][:, 2 * P:2 * P + NE], center[:, :], gw_sb[:, :], start=True, stop=True).then_inc(s_prep, 1)
            pe.wait_ge(s_prepe, 2)

            def agg(u, Q, j):
                if j == 0:
                    pe.wait_ge(s_xs, Q + 1)
                    if not (isinstance(Q, int) and Q < 2):
                        pe.wait_ge(s_ae, Q - 1)
                i = mm(ps_agg[u % 2][:, j * P:(j + 1) * P], xs[:, u % 2, j * P:(j + 1) * P],
                       aq[:, u, j * P:(j + 1) * P], start=True, stop=True)
                if j == QUAD - 1:
                    i.then_inc(s_m1, 1)

            def turn_h(h, TQ):
                pe.wait_ge(s_th, SPQ * TQ + SPQ)
                if not (isinstance(TQ, int) and TQ < 1):
                    pe.wait_ge(s_x1, TQ)
                for j in range(QUAD):
                    i = nc.tensor.transpose(ps_ht[:, j * P:(j + 1) * P], HT[:, h, j * P:(j + 1) * P], ident[:, :])
                i.then_inc(s_ht, 1)

            def turn_x(h, TQ):
                pe.wait_ge(s_x1, TQ + 1)
                if not (isinstance(TQ, int) and TQ < 1):
                    pe.wait_ge(s_xe, TQ)
                for j in range(QUAD):
                    i = nc.tensor.transpose(ps_xt[:, j * P:(j + 1) * P], x1s[:, h, j * P:(j + 1) * P], ident[:, :])
                i.then_inc(s_xt, 1)

            def logits(h, TQ):
                pe.wait_ge(s_xe, TQ + 1)
                if not (isinstance(TQ, int) and TQ < 1):
                    pe.wait_ge(s_l1, TQ)
                for j in range(QUAD):
                    i = mm(ps_lg[:, j * NE:(j + 1) * NE], x1T[:, h, j * P:(j + 1) * P], gwc[:, :],
                           start=True, stop=True)
                i.then_inc(s_lg, 1)

            def steps(RQ, fresh, h_tile, TQ, agg_u, aggQ):
                bankr = ps_rnn[u_of[0] % 2]
                if not (isinstance(RQ, int) and RQ < 2):
                    pe.wait_ge(s_th, SPQ * (RQ - 1))
                i = mm(bankr[:, :], Ec[:, :], AX[:, bass.ds(SPQ * RQ, SPQ), :], start=True, stop=True,
                       skip_group_check=True)
                if fresh:
                    i.then_inc(s_rn, 1)
                for k in range(SPQ):
                    S = SPQ * RQ + k
                    if not (fresh and k == 0):
                        pe.wait_ge(s_th, S)
                        prev = HT[:, (u_of[0] + (0 if k else 1)) % 2, ((k - 1) % SPQ) * NB:((k - 1) % SPQ + 1) * NB]
                        mm(bankr[:, k * NB:(k + 1) * NB], Wh_sb[:, :], prev, start=False, stop=True,
                           skip_group_check=True).then_inc(s_rn, 1)
                    if TQ is not None:
                        if k == 0:
                            turn_h(h_tile, TQ)
                        if k == 3:
                            turn_x(h_tile, TQ)
                        if k == 6:
                            logits(h_tile, TQ)
                    if agg_u is not None and 1 <= k < 1 + QUAD:
                        agg(agg_u, aggQ, k - 1)

            u_of = [0]

            def b1(J):
                for u in range(UN):
                    for j in range(QUAD):
                        agg(u, UN * J + u, j)
            loop(pe, 0, NQ // UN, b1)
            pe.wait_ge(s_ae, NQ)

            def b2(J):
                for u in range(UN):
                    u_of[0] = u
                    start = isinstance(J, int) and J == 0 and u == 0
                    steps(UN * J + u, start, (u + 1) % 2, None if start else UN * J + u - 1,
                          None if start else (u - 1) % UN, NQ + UN * J + u - 1)
            loop(pe, 0, NQ // UN, b2)
            for j in range(QUAD):
                agg(UN - 1, 2 * NQ - 1, j)
            pe.wait_ge(s_ae, 2 * NQ)

            def b3(J):
                for u in range(UN):
                    u_of[0] = u
                    steps(NQ + UN * J + u, isinstance(J, int) and J == 0 and u == 0, (u + 1) % 2,
                          NQ + UN * J + u - 1, None, None)
            loop(pe, 0, NQ // UN, b3)
            turn_h(1, 2 * NQ - 1)
            turn_x(1, 2 * NQ - 1)
            logits(1, 2 * NQ - 1)

        @block.scalar
        def _(act):
            a = nc.scalar.activation
            act.wait_ge(s_prep, 1)
            nc.scalar.copy(eWcT[:, :], bank[7][:, 0:P]).then_inc(s_prepe, 1)
            act.wait_ge(s_prep, 2)
            nc.scalar.copy(Ec[:, :], bank[7][:, P:2 * P])
            nc.scalar.copy(gwc[:, :], bank[7][:, 2 * P:2 * P + NE]).then_inc(s_prepe, 1)

            def agg_out(u, Q, g, q):
                act.wait_ge(s_m1, Q + 1)
                nc.scalar.copy(AX[:, g * P:(g + 1) * P, bass.ds(QUAD * q, QUAD)],
                               ps_agg[u % 2][:, :].rearrange("p (b t) -> p t b", b=QUAD)).then_inc(s_ae, 1)

            def x1T_out(h, TQ):
                act.wait_ge(s_xt, TQ + 1)
                if not (isinstance(TQ, int) and TQ < 2):
                    act.wait_ge(s_lg, TQ - 1)
                nc.scalar.copy(x1T[:, h, :], ps_xt[:, :]).then_inc(s_xe, 1)

            def steps(u, RQ, TQ, aggu, aggQ, aggq):
                for k in range(SPQ):
                    S = SPQ * RQ + k
                    if k == 0 and not (isinstance(RQ, int) and RQ < 2):
                        act.wait_ge(s_ht, RQ - 1)
                    act.wait_ge(s_rn, S + 1)
                    a(HT[:, u % 2, k * NB:(k + 1) * NB], ps_rnn[u % 2][:, k * NB:(k + 1) * NB], ACT.Tanh,
                      bias=bcol[:, :]).then_inc(s_th, 1)
                    if k == 5 and TQ is not None:
                        x1T_out((u + 1) % 2, TQ)
                    if k == 6 and aggu is not None:
                        agg_out(aggu, aggQ, 1, aggq)

            def b1(J):
                for u in range(UN):
                    agg_out(u, UN * J + u, 0, UN * J + u)
            loop(act, 0, NQ // UN, b1)

            def b2(J):
                for u in range(UN):
                    start = isinstance(J, int) and J == 0 and u == 0
                    q = UN * J + u - 1
                    steps(u, UN * J + u, None if start else q, None if start else (u - 1) % UN, NQ + q, q)
            loop(act, 0, NQ // UN, b2)
            agg_out(UN - 1, 2 * NQ - 1, 1, NQ - 1)

            def b3(J):
                for u in range(UN):
                    steps(u, NQ + UN * J + u, NQ + UN * J + u - 1, None, None, None)
            loop(act, 0, NQ // UN, b3)
            x1T_out(1, 2 * NQ - 1)

        @block.vector
        def _(dve):
            v = nc.vector

            def stats(u, Q):
                n = Q + 1
                h = u % 2
                dve.wait_ge(s_ld[u], (Q - u) * 8 + 32)
                if not (isinstance(Q, int) and Q < 2):
                    dve.wait_ge(s_xs, Q - 1)
                for j in range(QUAD):
                    i = v.bn_stats(bnb[:, h, j, :], xq[:, u, j * P:(j + 1) * P])
                i.then_inc(s_bn, 1)
                dve.wait_ge(s_bn, n)
                v.tensor_reduce(nrm[:, h, :], aq[:, u, :].rearrange("p (b d) -> p b d", b=QUAD), AX_X, ALU.add)
                for j in range(QUAD):
                    i = v.bn_aggr(mv[:, h, j, :], bnb[:, h, j, :])
                i.then_inc(s_st, 1)

            def tile_a(u, h, TQ):
                dve.wait_ge(s_ht, TQ + 1)
                dve.wait_ge(s_x2[u], (TQ - u) * 8 + 32)
                if not (isinstance(TQ, int) and TQ < 2):
                    dve.wait_ge(s_keep, TQ - 1)
                    dve.wait_ge(s_xt, TQ - 1)
                v.tensor_tensor(x1s[:, h, :], ps_ht[:, :], x2r[:, u, :], ALU.add).then_inc(s_x1, 1)

            def tile_b(u, h, TQ):
                dve.wait_ge(s_x1, TQ + 1)
                for j in range(QUAD):
                    i = v.bn_stats(bnb2[:, h, j, :], x1s[:, h, j * P:(j + 1) * P])
                i.then_inc(s_b2, 1)
                hold(dve, s_b2, TQ + 1)
                if not (isinstance(TQ, int) and TQ < 2):
                    dve.wait_ge(s_r2, TQ - 1)
                for j in range(QUAD):
                    i = v.bn_aggr(mvs[:, h, j, :], bnb2[:, h, j, :])
                i.then_inc(s_v2, 1)

            def tile_c(u, h, TQ):
                dve.wait_ge(s_lg, TQ + 1)
                dve.wait_ge(s_r2, TQ + 1)
                v.tensor_tensor(lgs[:, h, :, :], ps_lg[:, 0:QUAD * NE].rearrange("p (i e) -> p i e", i=QUAD),
                                rs2[:, bass.ds(QUAD * TQ, QUAD)].rearrange("p (i o) -> p i o", o=1)
                                .broadcast_to([P, QUAD, NE]), ALU.mult).then_inc(s_l1, 1)
                dve.wait_ge(s_l1, TQ + 1)
                v.tensor_tensor(lgs[:, h, :, :], lgs[:, h, :, :],
                                gb_bc[:, :].rearrange("p (o e) -> p o e", o=1).broadcast_to([P, QUAD, NE]),
                                ALU.add).then_inc(s_l2, 1)
                hold(dve, s_l2, TQ + 1)
                if not (isinstance(TQ, int) and TQ < 2):
                    dve.wait_ge(s_kt, TQ - 1)
                for j in range(QUAD):
                    i = v.max(mx8[:, h, j, :], lgs[:, h, j, :])
                i.then_inc(s_mx, 1)
                hold(dve, s_mx, TQ + 1)
                for j in range(QUAD):
                    i = v.max_index(ix8[:, h, j, :], mx8[:, h, j, :], lgs[:, h, j, :])
                i.then_inc(s_ix, 1)

            def b1(J):
                for u in range(UN):
                    stats(u, UN * J + u)
            loop(dve, 0, NQ // UN, b1)
            dve.wait_ge(s_w, 16 * 6)

            def b2(J):
                for u in range(UN):
                    t = (u - 1) % UN, (u + 1) % 2, UN * J + u - 1
                    start = isinstance(J, int) and J == 0 and u == 0
                    if not start:
                        tile_a(*t)
                        tile_b(*t)
                    stats(u, NQ + UN * J + u)
                    if not start:
                        tile_c(*t)
            loop(dve, 0, NQ // UN, b2)

            def b3(J):
                for u in range(UN):
                    t = (u - 1) % UN, (u + 1) % 2, NQ + UN * J + u - 1
                    tile_a(*t)
                    tile_b(*t)
                    tile_c(*t)
            loop(dve, 0, NQ // UN, b3)
            t = UN - 1, 1, 2 * NQ - 1
            tile_a(*t)
            tile_b(*t)
            tile_c(*t)

        front.close()

        W1b = sb("W1b", [P, NE, F + 2])
        W2 = sb("W2", [P, NE, 2, P])
        b2k = sb("b2k", [P, P])
        b2hi = sb("b2hi", [P, P], BF16)
        b2mid = sb("b2mid", [P, P], BF16)
        b2lo = sb("b2lo", [P, P], BF16)
        b2s = sb("b2s", [P, P], BF16)
        sel = sb("sel", [P, NE, P], BF16)
        gm_bc = sb("gm_bc", [P, P])
        bt_bc = sb("bt_bc", [P, P])
        ones = sb("ones", [P, P], BF16)
        neg_tri = sb("neg_tri", [P, P], BF16)
        iota_e = sb("iota_e", [P, NE])
        iota_i = sb("iota_i", [P, NIT])
        tok = sb("tok", [P, P], I32)
        tokf = sb("tokf", [P, P], I32)
        e2 = sb("e2", [P, P])
        w_1 = sb("w_1", [P, P])
        M = sb("M", [P, NE, P], BF16)
        zeros = sb("zeros", [P, 512])
        cum = sb("cum", [P, NE, P])
        cend = sb("cend", [P, NE])
        cnt = sb("cnt", [P, NE])
        cnti = sb("cnti", [P, NE], I32)
        nbi = sb("nbi", [P, NE], I32)
        nb = sb("nb", [P, NE])
        iend = sb("iend", [P, NE])
        off = sb("off", [P, NE])
        posf = sb("posf", [P, P])
        pos1 = sb("pos1", [P, P], I32)
        cmp = sb("cmp", [1, NIT, NE - 1])
        etf = sb("etf", [1, NIT])
        et_act = sb("et_act", [1, 2, NIT], I32)
        et_pe = sb("et_pe", [1, 2, NIT], I32)
        R = sb("R", [P, UN, QUAD, W_B])
        zq = sb("zq", [P, 2, QUAD * P])
        xT = sb("xT", [P, 2, QUAD * P])
        wr = sb("wr", [P, 2, QUAD, F + 2])
        hs = sb("hs", [P, QUAD, 2 * P])
        fst = sb("fst", [P, QUAD, 6])
        fmv = sb("fmv", [P, QUAD, 2])
        fve = sb("fve", [P, QUAD])
        fsd = sb("fsd", [P, QUAD])
        frs = sb("frs", [P, QUAD])

        r_w, r_c, r_v, r_e, r_M, r_ps, r_b, r_pool = (sem("r_" + k) for k in ("w", "c", "v", "e", "M", "ps", "b", "pool"))
        r_b2 = sem("r_b2")
        ready = sem("ready")
        scat_a = sem("scat_a")
        e_ld = [sem(f"e_ld{i}") for i in range(UN)]
        e_sc = [sem(f"e_sc{i}") for i in range(UN)]
        e_z, e_zt, e_xe, e_wc, e_h, e_r0, e_r1, e_o, e_acc, e_bn, e_ag, e_ve, e_sd, e_f1, e_f2, e_fin, e_rs = (
            sem("e_" + k) for k in ("z", "zt", "xe", "wc", "h", "r0", "r1", "o", "acc", "bn", "ag", "ve", "sd", "f1",
                                    "f2", "fin", "rs"))

        out_rows = out.rearrange("b l d -> (b l) d")
        qa = dram_a.ap().rearrange("(q j p) w -> p q j w", p=P, j=QUAD)
        qb = dram_b.ap().rearrange("(q j p) w -> p q j w", p=P, j=QUAD)
        ps_z, ps_h, ps_o = bank[0], (bank[1:3], bank[3:5]), bank[5:7]

        scrap = sb("scrap", [P, 1])
        limit = {}

        def scatter(dst, idx, src, n):
            return nc.gpsimd.indirect_dma_start(dst, bass.IndirectOffsetOnAxis(ap=idx, axis=0), src, None,
                                                bounds_check=limit[n], oob_is_err=False)

        with nc.Block() as block:
            def passes(eng, body):
                for r in range(2):
                    n = NQUAD // UN
                    for u in range(UN):
                        body(r, u, u + NQUAD * r, u, False)
                    with eng.Fori(1, n - 1) as J:
                        for u in range(UN):
                            body(r, UN * J + u, UN * J + u + NQUAD * r, u, False)
                    for u in range(UN):
                        q = NQUAD - UN + u
                        body(r, q, q + NQUAD * r, u, u == UN - 1)

            @block.sync
            def _(sp):
                for k in range(3):
                    sp.dma_start(b2k[k * NE:(k + 1) * NE, :], b2).then_inc(r_b2, 16)
                for c in range(2):
                    sp.dma_start(W1b[:, :, F + c], b1.rearrange("e (c f) -> c f e", c=2)[c],
                                 allow_slow_non_contiguous=True).then_inc(r_w, 16)
                sp.dma_start(W1b[:, :, 0:F], w1.rearrange("e h f -> h e f")).then_inc(r_w, 16)
                sp.dma_start(W2[:, :, :, :], w2.rearrange("e (c f) h -> f e c h", c=2)).then_inc(r_w, 16)
                for dst, src in ((gm_bc, gamma), (bt_bc, beta)):
                    sp.dma_start(dst[:, :], src.rearrange("(o e) -> o e", o=1).broadcast_to([P, P])).then_inc(r_w, 16)

                def quad(r, q, G, u, last):
                    if isinstance(q, int) and q == 0:
                        sp.wait_ge(scat_a, 16 * P)
                    if not (isinstance(G, int) and G < UN):
                        sp.wait_ge(e_sc[u], 16 * (G - u))
                    if r == 0:
                        sp.dma_start(R[:, u, :, 0:W_A], qa[:, bass.ds(q, 1), :, :].rearrange("p o j w -> p (o j) w")
                                     ).then_inc(e_ld[u], 16)
                    else:
                        sp.dma_start(R[:, u, :, :], qb[:, bass.ds(q, 1), :, :].rearrange("p o j w -> p (o j) w")
                                     ).then_inc(e_ld[u], 16)

                for r in range(2):
                    if r == 0:
                        for u in range(UN):
                            quad(r, u, u, u, False)
                    else:
                        for u in range(UN):
                            sp.wait_ge(e_sc[u], 16 * NQUAD)
                    with sp.Fori(1 - r, NQUAD // UN) as J:
                        for u in range(UN):
                            quad(r, UN * J + u, UN * J + u + NQUAD * r, u, False)
                for u in range(UN):
                    sp.wait_ge(e_sc[u], 16 * 2 * NQUAD)

            @block.gpsimd
            def _(pool):
                g = nc.gpsimd
                g.memset(ones[:, :], 1.0).then_inc(r_pool, 1)
                g.memset(neg_tri[:, :], -1.0).then_inc(r_pool, 1)
                g.memset(zeros[:, :], 0.0)
                pool.wait_ge(r_pool, 2)
                g.affine_select(out=neg_tri[:, :], in_=neg_tri[:, :], compare_op=ALU.is_ge, fill=0.0, base=0,
                                pattern=[[-1, P]], channel_multiplier=1)
                g.iota(iota_e[:, :], [[1, NE]], base=0, channel_multiplier=0, allow_small_or_imprecise_dtypes=True)
                g.iota(iota_i[:, :], [[1, NIT]], base=-1, channel_multiplier=0,
                       allow_small_or_imprecise_dtypes=True).then_inc(r_pool, 1)
                pool.wait_ge(r_pool, 3)
                for tp in range(2):
                    g.iota(tok[tp * NB:(tp + 1) * NB, :].rearrange("p (g i) -> p g i", g=GROUPS),
                           [[NB * P, GROUPS], [2, NB]], base=tp, channel_multiplier=P).then_inc(r_pool, 1)
                    pool.wait_ge(r_pool, 4 + tp)
                g.memset(sel[:, :, :], 0.0).then_inc(r_c, 1)
                pool.wait_ge(r_c, 1)
                g.tensor_copy(rows[:, :, C_TOKEN].bitcast(I32), tok[:, :]).then_inc(r_pool, 1)
                for k in range(3):
                    g.affine_select(out=sel[:, :, :], in_=sel[:, :, :], compare_op=ALU.not_equal, fill=1.0,
                                    base=-NE * k, pattern=[[-1, NE], [0, P]],
                                    channel_multiplier=1).then_inc(r_pool, 1)
                    pool.wait_ge(r_pool, 7 + k)

                for n in (NBLK * P, P * P):
                    limit[n] = pool.to_reg(n - 1)
                pool.wait_ge(ready, 1)
                pool.wait_ge(s_fill, 16 * 16)
                for t in range(P):
                    scatter(dram_a.ap(), pos1[:, t:t + 1], rows[:, t, :], NBLK * P).then_inc(scat_a, 16)

                def quad(r, q, G, u, last):
                    for j in range(QUAD):
                        if r == 0:
                            hold(pool, e_acc, QUAD * G + j + 1)
                            scatter(dram_b.ap(), R[:, u, j, C_POS2:C_POS2 + 1].bitcast(I32), R[:, u, j, :],
                                    NBLK * P).then_inc(e_sc[u], 16)
                        else:
                            if j == 0:
                                hold(pool, e_fin, G - NQUAD + 1)
                            scatter(out_rows, R[:, u, j, C_TOKEN:C_TOKEN + 1].bitcast(I32), R[:, u, j, W_A:W_B],
                                    P * P).then_inc(e_sc[u], 16)
                passes(pool, quad)

            @block.tensor
            def _(pe):
                mm = nc.tensor.matmul
                pe.wait_ge(r_c, 1)
                for r in range(2):
                    pe.wait_ge(r_M, r + 1)
                    if r == 1:
                        pe.wait_ge(r_b, 1)
                    for c in range(4):
                        mm(bank[c][:, :], ones[:, :], M[:, 4 * c:4 * c + 4, :].rearrange("p e t -> p (e t)"),
                           start=True, stop=True)
                        mm(bank[4 + c][:, :], neg_tri[:, :], M[:, 4 * c:4 * c + 4, :].rearrange("p e t -> p (e t)"),
                           start=True, stop=True).then_inc(r_ps, 1)
                pe.wait_ge(ready, 1)
                pe.wait_ge(r_w, 16 * 6)
                pe.wait_ge(r_v, 1)

                def turn(G, u):
                    pe.wait_ge(e_z, G + 1)
                    if not (isinstance(G, int) and G < 1):
                        pe.wait_ge(e_xe, G)
                    for j in range(QUAD):
                        i = nc.tensor.transpose(ps_z[:, j * P:(j + 1) * P], zq[:, u % 2, j * P:(j + 1) * P],
                                                ident[:, :])
                    i.then_inc(e_zt, 1)

                def first(G, u, j):
                    it = QUAD * G + j
                    if j == 0:
                        pe.wait_ge(e_xe, G + 1)
                    pe.wait_ge(e_wc, it + 1)
                    if not (isinstance(G, int) and G < 1 and j < 2):
                        pe.wait_ge(e_r0, it - 1)
                        pe.wait_ge(e_r1, it - 1)
                    for c in range(2):
                        i = mm(ps_h[c][j % 2][:, 0:P], wr[:, u % 2, j, c * P:(c + 1) * P],
                               xT[:, u % 2, j * P:(j + 1) * P], start=True, stop=True)
                    i.then_inc(e_h, 1)

                def second(G, u, j, e):
                    it = QUAD * G + j
                    if not (isinstance(G, int) and G < 1 and j < 2):
                        pe.wait_ge(e_acc, it - 1)
                    pe.wait_ge(e_r0, it + 1)
                    pe.wait_ge(e_r1, it + 1)
                    o = ps_o[j % 2][:, 0:P]
                    mm(o, sel[:, bass.ds(e, 1), :].rearrange("p o m -> p (o m)"), b2s[:, :], start=True, stop=False,
                       skip_group_check=True)
                    for c in range(2):
                        i = mm(o, hs[:, j, c * P:(c + 1) * P],
                               W2[:, bass.ds(e, 1), c, :].rearrange("p o f -> p (o f)"), start=False, stop=c == 1,
                               skip_group_check=True)
                    i.then_inc(e_o, 1)

                def quad(r, q, G, u, last):
                    e = [pe.value_load(et_pe[0:1, r, bass.ds(QUAD * q + j, 1)], min_val=0, max_val=NE - 1)
                         for j in range(QUAD)]
                    start = isinstance(q, int) and q == 0
                    if start:
                        turn(G, u)
                    for j in range(QUAD):
                        first(G, u, j)
                        if j == 2 and not last:
                            turn(G + 1, (u + 1) % UN)
                        if j:
                            second(G, u, j - 1, e[j])
                        elif not start:
                            second(G - 1, (u - 1) % UN, QUAD - 1, e[0])
                    if last:
                        second(G, u, QUAD - 1, pe.value_load(et_pe[0:1, r, QUAD * q + QUAD:QUAD * q + QUAD + 1],
                                                            min_val=0, max_val=NE - 1))
                passes(pe, quad)

            @block.scalar
            def _(act):
                a = nc.scalar.activation
                act.wait_ge(r_v, 1)
                a(e2[:, :], e2[:, :], ACT.Exp).then_inc(r_e, 1)
                act.wait_ge(ready, 1)
                act.wait_ge(r_w, 16 * 6)

                def turn_out(G, u):
                    act.wait_ge(e_zt, G + 1)
                    nc.scalar.copy(xT[:, u % 2, :], ps_z[:, :]).then_inc(e_xe, 1)

                def weights(G, u, j, e):
                    if not (isinstance(G, int) and G < 2):
                        act.wait_ge(e_h, QUAD * (G - 2) + j + 1)
                        act.wait_ge(e_r0, QUAD * (G - 2) + j + 1)
                    nc.scalar.copy(wr[:, u % 2, j, :], W1b[:, bass.ds(e, 1), :].rearrange("p o f -> p (o f)")
                                   ).then_inc(e_wc, 1)

                def relu(G, u, j):
                    it = QUAD * G + j
                    act.wait_ge(e_h, it + 1)
                    if not (isinstance(G, int) and G < 1):
                        act.wait_ge(e_o, it - 3)
                    a(hs[:, j, P:2 * P], ps_h[1][j % 2][:, 0:P], ACT.Relu, bias=wr[:, u % 2, j, F + 1:F + 2]
                      ).then_inc(e_r1, 1)

                def root(G):
                    n = G - NQUAD
                    act.wait_ge(e_ve, n + 1)
                    if not (isinstance(n, int) and n < 1):
                        act.wait_ge(e_rs, n)
                    a(fsd[:, :], fve[:, :], ACT.Sqrt).then_inc(e_sd, 1)

                def experts(r, q):
                    return [act.value_load(et_act[0:1, r, bass.ds(QUAD * q + j, 1)], min_val=0, max_val=NE - 1)
                            for j in range(QUAD)]

                def quad(r, q, G, u, last):
                    start = isinstance(q, int) and q == 0
                    if start:
                        for j, e in enumerate(experts(r, q)):
                            weights(G, u, j, e)
                        turn_out(G, u)
                    e = None if last else experts(r, q + 1)
                    for j in range(QUAD):
                        relu(G, u, j)
                        if not last:
                            weights(G + 1, (u + 1) % UN, j, e[j])
                        if j == 2 and not last:
                            turn_out(G + 1, (u + 1) % UN)
                        if j == 1 and r == 1 and not start:
                            root(G - 1)
                    if last and r == 1:
                        root(G)
                passes(act, quad)

            @block.vector
            def _(dve):
                v = nc.vector
                chain = sem("r_chain")
                n = [0]

                def link(i):
                    n[0] += 1
                    i.then_inc(chain, 1)
                    dve.wait_ge(chain, n[0])

                def bct(t, k=NE):
                    return t.rearrange("p (o t) -> p o t", o=1).broadcast_to([P, k, P])

                def bce(t):
                    return t.rearrange("p (e o) -> p e o", o=1).broadcast_to([P, NE, P])

                v.tensor_tensor(e2[:, :], top_v[:, :, 1], top_v[:, :, 0], ALU.subtract).then_inc(r_v, 1)
                dve.wait_ge(r_b2, 16 * 3)
                dve.wait_ge(r_c, 1)
                B = 3 * NE
                link(v.memset(b2s[:, :], 0.0))
                link(v.tensor_copy(b2hi[0:B, :], b2k[0:B, :]))
                link(v.tensor_tensor(b2k[0:B, :], b2k[0:B, :], b2hi[0:B, :], ALU.subtract))
                link(v.tensor_copy(b2mid[0:B, :], b2k[0:B, :]))
                link(v.tensor_tensor(b2k[0:B, :], b2k[0:B, :], b2mid[0:B, :], ALU.subtract))
                link(v.tensor_copy(b2lo[0:B, :], b2k[0:B, :]))
                link(v.tensor_copy(b2s[0:B, :], b2lo[0:B, :]))
                link(v.tensor_copy(b2s[0:2 * NE, :], b2mid[0:2 * NE, :]))
                link(v.tensor_copy(b2s[0:NE, :], b2hi[0:NE, :]))

                for r in range(2):
                    link(v.tensor_tensor(M[:, :, :], bce(iota_e[:, :]), bct(top_i[:, :, r]), ALU.is_equal))
                    v.memset(posf[:, 0:1], 0.0).then_inc(r_M, 1)
                    for c in range(4):
                        dve.wait_ge(r_ps, 4 * r + c + 1)
                        link(v.tensor_tensor_scan(cum[:, 4 * c:4 * c + 4, :].rearrange("p e t -> p (e t)"),
                                                  bank[c][:, :], zeros[:, :],
                                                  0.0 if c == 0 else cum[:, 4 * c - 1, P - 1:P], ALU.add, ALU.add))
                    link(v.tensor_copy(cend[:, :], cum[:, :, P - 1]))
                    link(v.tensor_copy(cnt[:, 0:1], cend[:, 0:1]))
                    link(v.tensor_tensor(cnt[:, 1:NE], cend[:, 1:NE], cend[:, 0:NE - 1], ALU.subtract))
                    link(v.tensor_scalar(cnti[:, :], cnt[:, :], float(P - 1), None, ALU.add))
                    link(v.tensor_scalar(nbi[:, :], cnti[:, :], 7, None, ALU.arith_shift_right))
                    link(v.tensor_copy(nb[:, :], nbi[:, :]))
                    link(v.tensor_tensor_scan(iend[:, :], nb[:, :], zeros[:, 0:NE], 0.0, ALU.add, ALU.add))
                    link(v.tensor_tensor(off[:, :], iend[:, :], nb[:, :], ALU.subtract))
                    link(v.tensor_scalar(off[:, :], off[:, :], float(P), None, ALU.mult))
                    link(v.tensor_tensor(off[:, :], off[:, :], cend[:, :], ALU.subtract))
                    link(v.tensor_tensor(off[:, :], off[:, :], cnt[:, :], ALU.add))
                    for e in range(NE):
                        i = v.scalar_tensor_tensor(out=cum[:, e, :], in0=cum[:, e, :], scalar=off[:, e:e + 1],
                                                   in1=bank[4 + e // 4][:, (e % 4) * P:(e % 4 + 1) * P],
                                                   op0=ALU.add, op1=ALU.add)
                    n[0] += 1
                    i.then_inc(chain, 1)
                    if r == 0:
                        v.memset(posf[:, 0:1], 0.0).then_inc(r_b, 1)
                    dve.wait_ge(chain, n[0])
                    link(v.tensor_tensor(cum[:, :, :], cum[:, :, :], M[:, :, :], ALU.mult))
                    link(v.tensor_reduce(posf[:, :], cum[:, :, :].rearrange("p e t -> p t e"), AX_X, ALU.add))
                    dst = pos1[:, :] if r == 0 else rows[:, :, C_POS2].bitcast(I32)
                    link(v.tensor_copy(dst, posf[:, :]))
                    link(v.tensor_tensor(cmp[:, :, :],
                                         iota_i[0:1, :].rearrange("p (i o) -> p i o", o=1)
                                         .broadcast_to([1, NIT, NE - 1]),
                                         iend[0:1, 0:NE - 1].rearrange("p (o e) -> p o e", o=1)
                                         .broadcast_to([1, NIT, NE - 1]), ALU.is_ge))
                    link(v.tensor_reduce(etf[:, :], cmp[:, :, :], AX_X, ALU.add))
                    link(v.tensor_copy(et_pe[:, r, :], etf[:, :]))
                    link(v.tensor_copy(et_act[:, r, 0:NIT - 1], etf[:, 1:NIT]))
                dve.wait_ge(r_e, 1)
                link(v.tensor_scalar(w_1[:, :], e2[:, :], 1.0, None, ALU.add))
                link(v.reciprocal(w_1[:, :], w_1[:, :]))
                link(v.tensor_tensor(rows[:, :, C_W2], w_1[:, :], e2[:, :], ALU.mult))
                link(v.tensor_copy(rows[:, :, C_W1], w_1[:, :]))
                link(v.tensor_copy(rows[:, :, C_RSTD], rs2[:, :]))
                link(v.tensor_tensor(e2[:, :], mv2[:, :, 0], rs2[:, :], ALU.mult))
                link(v.tensor_scalar(rows[:, :, C_NMR], e2[:, :], -1.0, None, ALU.mult))
                dve.wait_ge(r_pool, 9)
                dve.wait_ge(r_w, 16 * 6)
                v.memset(posf[:, 0:1], 0.0).then_inc(ready, 1)

                def zed(r, G, u):
                    dve.wait_ge(e_ld[u], 4 * (G - u) + 16)
                    if not (isinstance(G, int) and G < 2):
                        dve.wait_ge(e_zt, G - 1)
                        dve.wait_ge(e_acc, QUAD * G - QUAD)
                    for j in range(QUAD):
                        i = v.tensor_scalar(zq[:, u % 2, j * P:(j + 1) * P], R[:, u, j, 0:P],
                                            R[:, u, j, C_RSTD:C_RSTD + 1], R[:, u, j, C_NMR:C_NMR + 1],
                                            ALU.mult, ALU.add)
                    i.then_inc(e_z, 1)

                def relu(G, u, j):
                    it = QUAD * G + j
                    dve.wait_ge(e_h, it + 1)
                    if not (isinstance(G, int) and G < 1):
                        dve.wait_ge(e_o, it - 3)
                    v.tensor_scalar(hs[:, j, 0:P], ps_h[0][j % 2][:, 0:P], wr[:, u % 2, j, F:F + 1], 0.0, ALU.add,
                                    ALU.max).then_inc(e_r0, 1)

                def share(r, G, u, j):
                    it = QUAD * G + j
                    dve.wait_ge(e_o, it + 1)
                    w = C_W2 if r else C_W1
                    y = R[:, u, j, W_A:W_B]
                    v.scalar_tensor_tensor(out=y, in0=ps_o[j % 2][:, 0:P], scalar=R[:, u, j, w:w + 1],
                                           in1=y if r else zq[:, u % 2, j * P:(j + 1) * P], op0=ALU.mult,
                                           op1=ALU.add).then_inc(e_acc, 1)

                def norm_a(G, u):
                    m = G - NQUAD
                    hold(dve, e_acc, QUAD * G + QUAD)
                    for j in range(QUAD):
                        i = v.bn_stats(fst[:, j, :], R[:, u, j, W_A:W_B])
                    i.then_inc(e_bn, 1)
                    hold(dve, e_bn, m + 1)
                    v.memset(scrap[:, :], 0.0)
                    for j in range(QUAD):
                        i = v.bn_aggr(fmv[:, j, :], fst[:, j, :])
                    i.then_inc(e_ag, 1)
                    dve.wait_ge(e_ag, m + 1)
                    v.tensor_scalar(fve[:, :], fmv[:, :, 1], LN_EPS, None, ALU.add).then_inc(e_ve, 1)

                def norm_b(G, u):
                    m = G - NQUAD
                    for j in range(QUAD):
                        y = R[:, u, j, W_A:W_B]
                        i = v.scalar_tensor_tensor(out=y, in0=y, scalar=fmv[:, j, 0:1], in1=gm_bc[:, :],
                                                   op0=ALU.subtract, op1=ALU.mult)
                    i.then_inc(e_f1, 1)
                    dve.wait_ge(e_sd, m + 1)
                    v.reciprocal(frs[:, :], fsd[:, :]).then_inc(e_rs, 1)
                    dve.wait_ge(e_rs, m + 1)
                    dve.wait_ge(e_f1, m + 1)
                    for j in range(QUAD):
                        y = R[:, u, j, W_A:W_B]
                        i = v.scalar_tensor_tensor(out=y, in0=y, scalar=frs[:, j:j + 1], in1=R[:, u, j, 0:P],
                                                   op0=ALU.mult, op1=ALU.add)
                    i.then_inc(e_f2, 1)
                    dve.wait_ge(e_f2, m + 1)
                    y = R[:, u, :, W_A:W_B]
                    v.tensor_tensor(y, y, bt_bc[:, :].rearrange("p (o d) -> p o d", o=1).broadcast_to([P, QUAD, P]),
                                    ALU.add).then_inc(e_fin, 1)

                def quad(r, q, G, u, last):
                    start = isinstance(q, int) and q == 0
                    if start:
                        zed(r, G, u)
                    for j in range(QUAD):
                        relu(G, u, j)
                        if j:
                            share(r, G, u, j - 1)
                        elif not start:
                            share(r, G - 1, (u - 1) % UN, QUAD - 1)
                            if r:
                                norm_a(G - 1, (u - 1) % UN)
                        if j == 0 and not last:
                            zed(r, G + 1, (u + 1) % UN)
                        if j == 2 and r and not start:
                            norm_b(G - 1, (u - 1) % UN)
                    if last:
                        share(r, G, u, QUAD - 1)
                        if r:
                            norm_a(G, u)
                            norm_b(G, u)
                passes(dve, quad)


_INS = ['x', 'adj', 'L0_gnn_e_weight', 'L0_gnn_Wx', 'L0_gnn_Wh', 'L0_gnn_b', 'L0_ffn_gate_w', 'L0_ffn_gate_b',
        'L0_ffn_w1', 'L0_ffn_b1', 'L0_ffn_w2', 'L0_ffn_b2', 'L0_ffn_gamma', 'L0_ffn_beta']


def kernel(**inputs):
    import numpy as _np
    import concourse.bacc as _bacc
    from concourse import mybir as _mybir
    from concourse.bass_utils import run_bass_kernel_spmd as _run

    nc = _bacc.Bacc("TRN2", target_bir_lowering=False, num_devices=1)
    arrays, args = {}, []
    for name in _INS:
        a = _np.ascontiguousarray(inputs[name])
        arrays[f"in_{name}_dram"] = a
        args.append(nc.dram_tensor(f"in_{name}_dram", a.shape, _mybir.dt.from_np(a.dtype), kind="ExternalInput").ap())
    args.append(nc.dram_tensor("out_0_dram", inputs['x'].shape, F32, kind="ExternalOutput").ap())
    build(nc, *args)
    r = _run(nc, [arrays], core_ids=[0])
    return r.results[0]["out_0_dram"]
```

```python
from contextlib import ExitStack

import concourse.bass as bass
from concourse import mybir

F32 = mybir.dt.float32
BF16 = mybir.dt.bfloat16
I32 = mybir.dt.int32
U32 = mybir.dt.uint32
ALU = mybir.AluOpType
ACT = mybir.ActivationFunctionType
AX_X = mybir.AxisListType.X

P = 128
QUAD = 4
NQ = P // QUAD
SLOTS = 8
UN = 4
GNN_EPS = 1e-7
LN_EPS = 1e-5
C_RSTD, C_NMR, C_W1, C_W2, C_E2, C_RANK2, C_TOKEN, C_POS2 = range(P, P + 8)
W_A = C_POS2
C_Z, C_Y = P + 8, P + 8 + P
W_B = C_Y + P
NOWHERE = 1 << 16


def build(nc, x, adj, eW, Wx, Wh, b, gate_w, gate_b, w1, b1, w2, b2, gamma, beta, out):
    NE, _, F = w1.shape
    NBLK = P + NE
    NQUAD = NBLK // QUAD
    RING = 6
    NIT = NBLK + 8
    CAP = P * P + P
    SHIFT = 4096
    ROWS_A = NE * CAP + NE * P
    with ExitStack() as ctx:
        def sb(name, shape, dt=F32):
            return ctx.enter_context(nc.sbuf_tensor(name, shape, dt))

        front = ExitStack()

        def fsb(name, shape, dt=F32):
            return front.enter_context(nc.sbuf_tensor(name, shape, dt))

        def sem(name):
            return ctx.enter_context(nc.semaphore(name))

        bank = [ctx.enter_context(nc.psum_tensor(f"bank{i}", [P, 512], F32)) for i in range(8)]
        ps_agg = bank[0:2]
        ps_rnn = bank[2:4]
        ps_ht, ps_xt, ps_lg = bank[4], bank[5], bank[6]

        ident = sb("ident", [P, P])
        mhalf = sb("mhalf", [P, 2 * QUAD])
        eps_ln = sb("eps_ln", [P, 2 * QUAD])
        posr = sb("posr", [P, 2, QUAD + 1, 2 * NE])
        base = sb("base", [P, 2 * NE])
        iota_e = sb("iota_e", [P, QUAD * 2 * NE])
        iota_i = sb("iota_i", [P, NIT])
        ones = sb("ones", [P, P], BF16)
        tri = sb("tri", [P, P], BF16)
        tok = sb("tok", [P, P], I32)
        cnt = sb("cnt", [P, 2 * NE])
        cnti = sb("cnti", [P, 2 * NE], I32)
        nbi = sb("nbi", [P, 2 * NE], I32)
        nb = sb("nb", [P, 2, NE])
        zeros = sb("zeros", [P, NE])
        iend = sb("iend", [P, 2, NE])
        start2 = sb("start2", [P, NE])
        stride1 = sb("stride1", [P, NE])
        cmp = sb("cmp", [1, NIT, NE])
        etf = sb("etf", [1, NIT])
        vi = sb("vi", [1, NIT], I32)
        sti = sb("sti", [1, NIT], I32)
        padi = sb("padi", [1, NE], I32)
        et_act = sb("et_act", [1, 2, NIT], I32)
        et_pe = sb("et_pe", [1, 2, NIT], I32)
        W1b = sb("W1b", [P, NE, F + 2])
        W2 = sb("W2", [P, NE, 2, P])
        b2k = sb("b2k", [P, P])
        b2hi = sb("b2hi", [P, P], BF16)
        b2mid = sb("b2mid", [P, P], BF16)
        b2lo = sb("b2lo", [P, P], BF16)
        b2s = sb("b2s", [P, P], BF16)
        b2m = sb("b2m", [P, 1])
        w2m = sb("w2m", [P, 1])
        sel = sb("sel", [P, NE, P], BF16)
        gm_bc = sb("gm_bc", [P, P])
        bt_bc = sb("bt_bc", [P, P])
        filler = sb("filler", [P, W_B])
        center = fsb("center", [P, P])
        eW_sb = fsb("eW_sb", [P, P])
        Wx_sb = fsb("Wx_sb", [P, P])
        Wh_sb = fsb("Wh_sb", [P, P])
        bcol = fsb("bcol", [P, 1])
        gw_sb = fsb("gw_sb", [P, NE])
        gb_bc = fsb("gb_bc", [P, NE])
        eWcT = fsb("eWcT", [P, P])
        Ec = fsb("Ec", [P, P])
        gwc = fsb("gwc", [P, NE])
        xq = fsb("xq", [P, SLOTS, QUAD * P])
        aq = fsb("aq", [P, SLOTS, QUAD * P])
        xs = fsb("xs", [P, 2, QUAD * P])
        AX = fsb("AX", [P, P, P])
        HT = fsb("HT", [P, 2, QUAD * P])
        x2r = fsb("x2r", [P, UN, QUAD * P])
        st = fsb("st", [P, SLOTS, QUAD, W_A])
        idx1 = fsb("idx1", [P, SLOTS, QUAD], I32)
        dd = fsb("dd", [P, 2, QUAD])
        ex = fsb("ex", [P, 2, QUAD])
        den = fsb("den", [P, QUAD])
        hot = fsb("hot", [P, 2, (QUAD + 1) * 2 * NE], BF16)
        picked = fsb("picked", [P, QUAD * 2, NE])
        place = fsb("place", [P, QUAD, 2])
        x1T = fsb("x1T", [P, 2, QUAD * P])
        bnb = fsb("bnb", [P, SLOTS, QUAD, 6])
        mv = fsb("mv", [P, SLOTS, QUAD, 2])
        nrm = fsb("nrm", [P, SLOTS, QUAD])
        sc = fsb("sc", [P, 5, 2 * QUAD])
        scq = fsb("scq", [P, SLOTS, QUAD])
        bnb2 = fsb("bnb2", [P, 2, QUAD, 6])
        ve2 = fsb("ve2", [P, 2, QUAD])
        lgs = fsb("lgs", [P, 2, QUAD, NE])
        mvs = fsb("mvs", [P, 2, QUAD, 2])
        mx8 = fsb("mx8", [P, 2, QUAD, 8])
        ix8 = fsb("ix8", [P, 2, QUAD, 8], U32)

        weights_in_front = sem("weights_in_front")
        constants_ready = sem("constants_ready")
        fold_products = sem("fold_products")
        fold_copied = sem("fold_copied")
        pool_step = sem("pool_step")
        x_stats = sem("x_stats")
        row_stats_ready = sem("row_stats_ready")
        scales_ready = sem("scales_ready")
        scaled_x_ready = sem("scaled_x_ready")
        aggregated = sem("aggregated")
        aggregate_copied = sem("aggregate_copied")
        step_summed = sem("step_summed")
        state_ready = sem("state_ready")
        states_turned = sem("states_turned")
        x1_ready = sem("x1_ready")
        x1_stats = sem("x1_stats")
        x1_moments = sem("x1_moments")
        x1_var_ready = sem("x1_var_ready")
        x1_rstd_ready = sem("x1_rstd_ready")
        x1_nmr_ready = sem("x1_nmr_ready")
        x1_turned = sem("x1_turned")
        x1T_ready = sem("x1T_ready")
        logits_done = sem("logits_done")
        logits_scaled = sem("logits_scaled")
        logits_ready = sem("logits_ready")
        top_values_ready = sem("top_values_ready")
        top_indices_ready = sem("top_indices_ready")
        top_gap_ready = sem("top_gap_ready")
        top_exp_ready = sem("top_exp_ready")
        softmax_step = sem("softmax_step")
        gate_weights_ready = sem("gate_weights_ready")
        one_hots_ready = sem("one_hots_ready")
        counts_done = sem("counts_done")
        places_ready = sem("places_ready")
        places_picked = sem("places_picked")
        place_ready = sem("place_ready")
        rows_ready = sem("rows_ready")
        table_step = sem("table_step")
        vector_step = sem("vector_step")
        surplus_filled = sem("surplus_filled")
        filler_ready = sem("filler_ready")
        padded = sem("padded")
        ends_known = sem("ends_known")
        tables_ready = sem("tables_ready")
        w1_loaded = sem("w1_loaded")
        w2_loaded = sem("w2_loaded")
        routing_ready = sem("routing_ready")
        pool_built = sem("pool_built")
        w2_centred = sem("w2_centred")
        second_filled = sem("second_filled")
        z_ready = sem("z_ready")
        z_turned = sem("z_turned")
        zT_ready = sem("zT_ready")
        w1_copied = sem("w1_copied")
        hidden_done = sem("hidden_done")
        relu0_done = sem("relu0_done")
        relu1_done = sem("relu1_done")
        output_done = sem("output_done")
        share_added = sem("share_added")
        second_step = sem("second_step")
        x1_beta_ready = sem("x1_beta_ready")
        y_stats = sem("y_stats")
        y_moments = sem("y_moments")
        y_var_ready = sem("y_var_ready")
        y_std_ready = sem("y_std_ready")
        y_rstd_ready = sem("y_rstd_ready")
        y_scaled = sem("y_scaled")
        result_ready = sem("result_ready")
        batches_loaded = [sem(f"batches_loaded{i}") for i in range(SLOTS)]
        tiles_loaded = [sem(f"tiles_loaded{i}") for i in range(UN)]
        rows_sent = [sem(f"rows_sent{i}") for i in range(SLOTS)]
        blocks_loaded = [sem(f"blocks_loaded{i}") for i in range(RING)]
        blocks_sent = [sem(f"blocks_sent{i}") for i in range(RING)]

        dram_a = nc.dram_tensor("rows_by_first", [ROWS_A, W_A], F32)
        dram_b = nc.dram_tensor("rows_by_second", [NBLK * P, W_B], F32)

        qb_rows = dram_b.ap().rearrange("(i p) w -> p i w", p=P)
        x_bt = x.rearrange("b l d -> l b d")
        a_bt = adj.rearrange("b l m -> l b m")

        block = front.enter_context(nc.Block())

        def hold(eng, semaphore, value):
            value = value if isinstance(value, int) else eng.to_reg(value)
            eng.wait_ge(constants_ready, 1)
            eng.wait_ge(semaphore, value)

        regs = {}

        def numbers(eng, table, most=NE - 1):
            n = regs[id(eng)] = regs.get(id(eng), 0) + 1
            four = [eng.alloc_register(f"expert{n}_{j}") for j in range(QUAD)]
            eng.reg_load(four, table)
            return [bass.RuntimeValue.of_register_unchecked(k).with_bounds(min_val=0, max_val=most) for k in four]

        def pad(eng, e0):
            for e in (e0, e0 + 4):
                for row in numbers(eng, padi[0:1, e:e + 4], NE * CAP - P):
                    eng.dma_start(dram_a.ap()[bass.ds(row, P), :], filler[:, 0:W_A]).then_inc(padded, 16)

        limit = {}

        def scatter(dst, idx, src, n):
            return nc.gpsimd.indirect_dma_start(dst, bass.IndirectOffsetOnAxis(ap=idx, axis=0), src, None,
                                                bounds_check=limit[n], oob_is_err=False)

        def beyond(q, n):
            return not (isinstance(q, int) and q < n)

        def quads(eng, body, n=UN):
            for u in range(n):
                body(u, u)
            with eng.Fori(1, NQ // n) as J:
                for u in range(n):
                    body(n * J + u, u)

        @block.sync
        def _(sp):
            for dst, src in ((eW_sb[:, :], eW), (Wx_sb[:, :], Wx), (Wh_sb[:, :], Wh),
                             (gw_sb[:, :], gate_w), (bcol[:, :], b.rearrange("(u o) -> u o", o=1)),
                             (gb_bc[:, :], gate_b.rearrange("(o e) -> o e", o=1).broadcast_to([P, NE]))):
                sp.dma_start(dst, src).then_inc(weights_in_front, 16)

            def batches(q, u):
                if beyond(q, SLOTS):
                    sp.wait_ge(aggregated, q - SLOTS + 1)
                sp.dma_start(xq[:, u, :].rearrange("p (b d) -> p b d", b=QUAD),
                             x_bt[:, bass.ds(QUAD * q, QUAD), :]).then_inc(batches_loaded[u], 16)
                sp.dma_start(aq[:, u, :].rearrange("p (b d) -> p b d", b=QUAD),
                             a_bt[:, bass.ds(QUAD * q, QUAD), :]).then_inc(batches_loaded[u], 16)

            def tiles(q, u):
                if beyond(q, UN):
                    sp.wait_ge(x1_ready, q - UN + 1)
                sp.dma_start(x2r[:, u, :].rearrange("p (i d) -> p i d", i=QUAD),
                             x[:, bass.ds(QUAD * q, QUAD), :]).then_inc(tiles_loaded[u], 16)

            def filled(dst, w, n):
                return sp.dma_start(dst.rearrange("(i p) w -> p i w", p=P),
                                    filler[:, 0:w].rearrange("p (o w) -> p o w", o=1).broadcast_to([P, n, w]))

            quads(sp, batches, SLOTS)
            for u in range(UN):
                tiles(u, u)
            for k in range(3):
                sp.dma_start(b2k[k * NE:(k + 1) * NE, :], b2).then_inc(w2_loaded, 16)
            sp.dma_start(W2[:, :, :, :], w2.rearrange("e (c f) h -> f e c h", c=2)).then_inc(w2_loaded, 16)
            sp.wait_ge(filler_ready, 1)
            filled(dram_a.ap()[NE * CAP:ROWS_A, :], W_A, NE).then_inc(surplus_filled, 16)
            for u in range(UN):
                tiles(UN + u, u)
            sp.dma_start(W1b[:, :, 0:F], w1.rearrange("e h f -> h e f")).then_inc(w1_loaded, 16)
            for c in range(2):
                sp.dma_start(W1b[:, :, F + c], b1.rearrange("e (c f) -> c f e", c=2)[c],
                             allow_slow_non_contiguous=True).then_inc(w1_loaded, 16)
            for dst, src in ((gm_bc, gamma), (bt_bc, beta)):
                sp.dma_start(dst[:, :], src.rearrange("(o e) -> o e", o=1).broadcast_to([P, P])).then_inc(w1_loaded, 16)
            n = NBLK // 6
            with sp.Fori(2, NQ // UN) as J:
                for u in range(UN):
                    tiles(UN * J + u, u)
                filled(dram_b.ap()[bass.ds(n * P * (J - 2), n * P), :], W_B, n).then_inc(second_filled, 16)
            sp.wait_ge(ends_known, 1)
            pad(sp, 0)

        @block.gpsimd
        def _(pool):
            g = nc.gpsimd
            g.memset(ident[:, :], 0.0).then_inc(pool_step, 1)
            g.memset(mhalf[:, :], -0.5)
            g.memset(eps_ln[:, :], LN_EPS)
            pool.wait_ge(pool_step, 1)
            g.affine_select(out=ident[:, :], in_=ident[:, :], compare_op=ALU.not_equal, fill=1.0, base=0,
                            pattern=[[-1, P]], channel_multiplier=1).then_inc(pool_step, 1)
            pool.wait_ge(pool_step, 2)
            g.tensor_scalar(center[:, :], ident[:, :], -1.0 / P, None, ALU.add).then_inc(constants_ready, 1)
            g.memset(filler[:, :], 0.0).then_inc(pool_step, 1)
            pool.wait_ge(pool_step, 3)
            g.iota(filler[:, C_TOKEN:C_TOKEN + 1].bitcast(I32), [[0, 1]], base=NOWHERE, channel_multiplier=1)
            g.iota(filler[:, C_RANK2:C_RANK2 + 1], [[0, 1]], base=NOWHERE, channel_multiplier=1,
                   allow_small_or_imprecise_dtypes=True).then_inc(filler_ready, 1)

            def scale(q, u):
                if u % 2 == 0:
                    return
                n = 3 * ((q + 1) // 2)
                pool.wait_ge(row_stats_ready, q + 1)
                g.tensor_tensor(sc[:, 1, :], mv[:, u - 1:u + 1, :, 1].rearrange("p u j -> p (u j)"), eps_ln[:, :], ALU.add)
                g.tensor_scalar(sc[:, 0, :], nrm[:, u - 1:u + 1, :].rearrange("p u j -> p (u j)"), GNN_EPS, None,
                                ALU.max).then_inc(pool_step, 1)
                pool.wait_ge(pool_step, n + 1)
                g.tensor_tensor(sc[:, 2, :], sc[:, 0, :], sc[:, 1, :], ALU.mult).then_inc(pool_step, 1)
                pool.wait_ge(pool_step, n + 2)
                g.tensor_tensor(sc[:, 3, :], sc[:, 0, :], sc[:, 2, :], ALU.mult).then_inc(pool_step, 1)
                pool.wait_ge(pool_step, n + 3)
                if beyond(q, SLOTS):
                    pool.wait_ge(scaled_x_ready, q - SLOTS + 1)
                g.tensor_tensor(scq[:, u - 1:u + 1, :].rearrange("p u j -> p (u j)"), sc[:, 3, :], mhalf[:, :],
                                ALU.pow).then_inc(scales_ready, 2)

            def rstd(q, u):
                h = u % 2
                pool.wait_ge(x1_var_ready, q + 1)
                g.tensor_tensor(st[:, u, :, C_RSTD], ve2[:, h, :], mhalf[:, 0:QUAD], ALU.pow).then_inc(x1_rstd_ready, 1)

            def send(q, u):
                hold(pool, rows_ready, q + 1)
                for j in range(QUAD):
                    scatter(dram_a.ap(), idx1[:, u, j:j + 1], st[:, u, j, :], ROWS_A).then_inc(rows_sent[u], 16)

            quads(pool, scale, SLOTS)
            for n in (NBLK * P, P * P, ROWS_A):
                limit[n] = pool.to_reg(n - 1)
            g.memset(ones[:, :], 1.0).then_inc(pool_built, 1)
            g.memset(tri[:, :], 1.0).then_inc(pool_built, 1)
            g.memset(posr[:, :, :, :], 0.0).then_inc(pool_built, 1)
            pool.wait_ge(pool_built, 3)
            g.affine_select(out=tri[:, :], in_=tri[:, :], compare_op=ALU.is_gt, fill=0.0, base=0,
                            pattern=[[1, P]], channel_multiplier=-1)
            g.iota(iota_e[:, :], [[0, 2 * QUAD], [1, NE]], base=0, channel_multiplier=0,
                   allow_small_or_imprecise_dtypes=True)
            g.iota(posr[:, 1, QUAD, 0:NE], [[CAP, NE]], base=0, channel_multiplier=0,
                   allow_small_or_imprecise_dtypes=True).then_inc(pool_built, 1)
            g.iota(tok[:, :], [[1, P]], base=0, channel_multiplier=P).then_inc(pool_built, 1)
            pool.wait_ge(pool_built, 5)
            g.tensor_copy(base[:, :], posr[:, 1, QUAD, :]).then_inc(routing_ready, 1)

            def rest():
                g.iota(iota_i[:, :], [[1, NIT]], base=-2, channel_multiplier=0,
                       allow_small_or_imprecise_dtypes=True)
                g.memset(sel[:, :, :], 0.0).then_inc(pool_built, 1)
                pool.wait_ge(pool_built, 6)
                for k in range(3):
                    g.affine_select(out=sel[:, :, :], in_=sel[:, :, :], compare_op=ALU.not_equal, fill=1.0,
                                    base=-NE * k, pattern=[[-1, NE], [0, P]],
                                    channel_multiplier=1).then_inc(pool_built, 1)
                    pool.wait_ge(pool_built, 7 + k)
            rest()

            def turn(q, u):
                if beyond(q, 1):
                    rstd(q - 1, (u - 1) % SLOTS)
                if beyond(q, 3):
                    send(q - 3, (u - 3) % SLOTS)
            quads(pool, turn, SLOTS)
            rstd(NQ - 1, SLOTS - 1)
            for k in range(3):
                send(NQ - 3 + k, SLOTS - 3 + k)

        @block.tensor
        def _(pe):
            mm = nc.tensor.matmul
            pe.wait_ge(weights_in_front, 16 * 6)
            pe.wait_ge(constants_ready, 1)
            mm(bank[7][:, 0:P], eW_sb[:, :], center[:, :], start=True, stop=True).then_inc(fold_products, 1)
            pe.wait_ge(fold_copied, 1)
            mm(bank[7][:, P:2 * P], eWcT[:, :], Wx_sb[:, :], start=True, stop=True)
            mm(bank[7][:, 2 * P:2 * P + NE], center[:, :], gw_sb[:, :], start=True, stop=True).then_inc(fold_products, 1)
            pe.wait_ge(fold_copied, 2)

            def agg(q, u):
                pe.wait_ge(scaled_x_ready, q + 1)
                if beyond(q, 2):
                    pe.wait_ge(aggregate_copied, q - 1)
                for j in range(QUAD):
                    i = mm(ps_agg[u % 2][:, j * P:(j + 1) * P], xs[:, u % 2, j * P:(j + 1) * P],
                           aq[:, u, j * P:(j + 1) * P], start=True, stop=True)
                i.then_inc(aggregated, 1)

            def turn_h(q, u):
                if beyond(q, 1):
                    pe.wait_ge(x1_ready, q)
                for j in range(QUAD):
                    i = nc.tensor.transpose(ps_ht[:, j * P:(j + 1) * P], HT[:, u % 2, j * P:(j + 1) * P], ident[:, :])
                i.then_inc(states_turned, 1)

            def turn_x(q, u):
                pe.wait_ge(x1_ready, q + 1)
                if beyond(q, 1):
                    pe.wait_ge(x1T_ready, q)
                for j in range(QUAD):
                    i = nc.tensor.transpose(ps_xt[:, j * P:(j + 1) * P], st[:, u % SLOTS, j, 0:P],
                                            ident[:, :])
                i.then_inc(x1_turned, 1)

            def logits(q, u):
                pe.wait_ge(x1T_ready, q + 1)
                if beyond(q, 1):
                    pe.wait_ge(logits_scaled, q)
                for j in range(QUAD):
                    i = mm(ps_lg[:, j * NE:(j + 1) * NE], x1T[:, u % 2, j * P:(j + 1) * P], gwc[:, :],
                           start=True, stop=True)
                i.then_inc(logits_done, 1)

            def count(q, u):
                pe.wait_ge(one_hots_ready, q + 1)
                if beyond(q, 2):
                    pe.wait_ge(places_ready, q - 1)
                o, w = ps_agg[u % 2], 2 * NE
                m = hot[:, u % 2, w:]
                mm(o[:, 0:5 * w], ones[:, :], hot[:, u % 2, :], start=True, stop=False, skip_group_check=True)
                mm(o[:, 0:4 * w], tri[:, :], m, start=False, stop=False, skip_group_check=True)
                for k in range(3, 0, -1):
                    i = mm(o[:, (5 - k) * w:5 * w], ones[:, :], m[:, 0:k * w], start=False, stop=k == 1,
                           skip_group_check=True)
                i.then_inc(counts_done, 1)

            def fresh(q, u):
                return mm(ps_rnn[u % 2][:, :], Ec[:, :], AX[:, bass.ds(QUAD * q, QUAD), :], start=True, stop=True,
                          skip_group_check=True)

            def steps(q, u):
                for k in range(QUAD):
                    if k or beyond(q, 1):
                        pe.wait_ge(state_ready, QUAD * q + k)
                        h = (u if k else u - 1) % 2
                        mm(ps_rnn[u % 2][:, k * P:(k + 1) * P], Wh_sb[:, :],
                           HT[:, h, ((k - 1) % QUAD) * P:((k - 1) % QUAD + 1) * P], start=False, stop=True,
                           skip_group_check=True).then_inc(step_summed, 1)
                    if k == 0 and not (isinstance(q, int) and q == NQ - 1):
                        fresh(q + 1, u + 1)
                    if k == 1 and beyond(q, 1):
                        turn_h(q - 1, u - 1)
                    if k == 2 and beyond(q, 3):
                        count(q - 3, u - 3)
                    if k == 2 and beyond(q, 2):
                        logits(q - 2, u - 2)
                    if k == 3 and beyond(q, 1):
                        turn_x(q - 1, u - 1)

            quads(pe, agg, SLOTS)
            pe.wait_ge(aggregate_copied, NQ)
            fresh(0, 0).then_inc(step_summed, 1)
            for u in range(SLOTS):
                steps(u, u)
            with pe.Fori(1, NQ // SLOTS - 1) as J:
                for u in range(SLOTS):
                    steps(SLOTS * J + u, u)
            for u in range(SLOTS):
                steps(NQ - SLOTS + u, u)
            pe.wait_ge(state_ready, P)
            turn_h(NQ - 1, UN - 1)
            count(NQ - 3, UN - 3)
            logits(NQ - 2, UN - 2)
            turn_x(NQ - 1, SLOTS - 1)
            logits(NQ - 1, UN - 1)
            count(NQ - 2, UN - 2)
            count(NQ - 1, UN - 1)

        @block.scalar
        def _(act):
            a = nc.scalar.activation
            act.wait_ge(fold_products, 1)
            nc.scalar.copy(eWcT[:, :], bank[7][:, 0:P]).then_inc(fold_copied, 1)
            act.wait_ge(fold_products, 2)
            nc.scalar.copy(Ec[:, :], bank[7][:, P:2 * P])
            nc.scalar.copy(gwc[:, :], bank[7][:, 2 * P:2 * P + NE]).then_inc(fold_copied, 1)

            def scaled(q, u):
                act.wait_ge(scales_ready, q + 1)
                act.wait_ge(batches_loaded[u], 32 * (q - u) // SLOTS + 32)
                if beyond(q, 2):
                    act.wait_ge(aggregated, q - 1)
                for j in range(QUAD):
                    i = a(xs[:, u % 2, j * P:(j + 1) * P], xq[:, u, j * P:(j + 1) * P], ACT.Identity,
                          scale=scq[:, u, j:j + 1])
                i.then_inc(scaled_x_ready, 1)

            def agg_out(q, u):
                act.wait_ge(aggregated, q + 1)
                nc.scalar.copy(AX[:, :, bass.ds(QUAD * q, QUAD)],
                               ps_agg[u % 2][:, :].rearrange("p (b t) -> p t b", b=QUAD)).then_inc(aggregate_copied, 1)

            def first(q, u):
                scaled(q, u)
                if beyond(q, 1):
                    agg_out(q - 1, u - 1)

            def x1T_out(q, u):
                act.wait_ge(x1_turned, q + 1)
                if beyond(q, 2):
                    act.wait_ge(logits_done, q - 1)
                nc.scalar.copy(x1T[:, u % 2, :], ps_xt[:, :]).then_inc(x1T_ready, 1)

            def exps(q, u):
                act.wait_ge(top_gap_ready, q + 1)
                if beyond(q, 2):
                    act.wait_ge(gate_weights_ready, q - 1)
                a(ex[:, u % 2, :], dd[:, u % 2, :], ACT.Exp).then_inc(top_exp_ready, 1)

            def steps(q, u):
                for k in range(QUAD):
                    if k == 0 and beyond(q, 2):
                        act.wait_ge(states_turned, q - 1)
                    act.wait_ge(step_summed, QUAD * q + k + 1)
                    a(HT[:, u % 2, k * P:(k + 1) * P], ps_rnn[u % 2][:, k * P:(k + 1) * P], ACT.Tanh,
                      bias=bcol[:, :]).then_inc(state_ready, 1)
                    if k == 0 and beyond(q, 2):
                        x1T_out(q - 2, u - 2)
                    if k == 1 and beyond(q, 3):
                        exps(q - 3, u - 3)

            quads(act, first, SLOTS)
            agg_out(NQ - 1, UN - 1)
            quads(act, steps)
            exps(NQ - 3, UN - 3)
            x1T_out(NQ - 2, UN - 2)
            x1T_out(NQ - 1, UN - 1)
            exps(NQ - 2, UN - 2)
            exps(NQ - 1, UN - 1)
            act.wait_ge(ends_known, 1)
            pad(act, 8)

        @block.vector
        def _(dve):
            v = nc.vector

            def stats(q, u):
                dve.wait_ge(batches_loaded[u], 32 * (q - u) // SLOTS + 32)
                if beyond(q, SLOTS):
                    dve.wait_ge(scales_ready, q - u % 2 - SLOTS + 2)
                for j in range(QUAD):
                    i = v.bn_stats(bnb[:, u, j, :], xq[:, u, j * P:(j + 1) * P])
                i.then_inc(x_stats, 1)
                dve.wait_ge(x_stats, q + 1)
                v.tensor_reduce(nrm[:, u, :], aq[:, u, :].rearrange("p (b d) -> p b d", b=QUAD), AX_X, ALU.add)
                for j in range(QUAD):
                    i = v.bn_aggr(mv[:, u, j, :], bnb[:, u, j, :])
                i.then_inc(row_stats_ready, 1)

            def tile_a(q, u):
                dve.wait_ge(states_turned, q + 1)
                dve.wait_ge(tiles_loaded[u % UN], 16 * (q - u % UN) // UN + 16)
                if beyond(q, SLOTS):
                    dve.wait_ge(rows_sent[u], 64 * (q - u) // SLOTS)
                v.tensor_tensor(st[:, u, :, 0:P], ps_ht[:, :].rearrange("p (i d) -> p i d", i=QUAD),
                                x2r[:, u % UN, :].rearrange("p (i d) -> p i d", i=QUAD), ALU.add).then_inc(x1_ready, 1)

            def tile_b(q, u):
                dve.wait_ge(x1_ready, q + 1)
                for j in range(QUAD):
                    i = v.bn_stats(bnb2[:, u % 2, j, :], st[:, u, j, 0:P])
                i.then_inc(x1_stats, 1)

            def tile_b2(q, u):
                if beyond(q, 2):
                    hold(dve, x1_nmr_ready, q - 1)
                hold(dve, x1_stats, q + 1)
                for j in range(QUAD):
                    i = v.bn_aggr(mvs[:, u % 2, j, :], bnb2[:, u % 2, j, :])
                i.then_inc(x1_moments, 1)

            def tile_b3(q, u):
                dve.wait_ge(x1_moments, q + 1)
                if beyond(q, 2):
                    dve.wait_ge(x1_rstd_ready, q - 1)
                v.tensor_scalar(ve2[:, u % 2, :], mvs[:, u % 2, :, 1], LN_EPS, None, ALU.add).then_inc(x1_var_ready, 1)

            def gate_1(q, u):
                h = u % 2
                dve.wait_ge(logits_done, q + 1)
                dve.wait_ge(x1_rstd_ready, q + 1)
                v.tensor_tensor(lgs[:, h, :, :], ps_lg[:, 0:QUAD * NE].rearrange("p (i e) -> p i e", i=QUAD),
                                st[:, u, :, C_RSTD:C_RSTD + 1].broadcast_to([P, QUAD, NE]), ALU.mult).then_inc(logits_scaled, 1)
                v.scalar_tensor_tensor(out=st[:, u, :, C_NMR], in0=mvs[:, h, :, 0], scalar=-1.0,
                                       in1=st[:, u, :, C_RSTD], op0=ALU.mult, op1=ALU.mult).then_inc(x1_nmr_ready, 1)

            def gate_2(q, u):
                h = u % 2
                dve.wait_ge(logits_scaled, q + 1)
                v.tensor_tensor(lgs[:, h, :, :], lgs[:, h, :, :],
                                gb_bc[:, :].rearrange("p (o e) -> p o e", o=1).broadcast_to([P, QUAD, NE]),
                                ALU.add).then_inc(logits_ready, 1)

            def gate_3(q, u):
                h = u % 2
                if beyond(q, 2):
                    hold(dve, one_hots_ready, q - 1)
                hold(dve, logits_ready, q + 1)
                for j in range(QUAD):
                    i = v.max(mx8[:, h, j, :], lgs[:, h, j, :])
                i.then_inc(top_values_ready, 1)

            def gate_4(q, u):
                h = u % 2
                hold(dve, top_values_ready, q + 1)
                for j in range(QUAD):
                    i = v.max_index(ix8[:, h, j, :], mx8[:, h, j, :], lgs[:, h, j, :])
                i.then_inc(top_indices_ready, 1)
                if beyond(q, 2):
                    dve.wait_ge(top_exp_ready, q - 1)
                v.tensor_tensor(dd[:, h, :], mx8[:, h, :, 1], mx8[:, h, :, 0], ALU.subtract).then_inc(top_gap_ready, 1)

            def gate_5(q, u):
                h = u % 2
                dve.wait_ge(top_indices_ready, q + 1)
                if beyond(q, 2):
                    dve.wait_ge(counts_done, q - 1)
                v.tensor_tensor(hot[:, h, 2 * NE:].rearrange("p (j r e) -> p j r e", j=QUAD, r=2),
                                ix8[:, h, :, 0:2].rearrange("p j (r o) -> p j r o", o=1)
                                .broadcast_to([P, QUAD, 2, NE]),
                                iota_e[:, :].rearrange("p (j r e) -> p j r e", j=QUAD, r=2), ALU.is_equal)
                v.tensor_copy(st[:, u, :, C_E2], ix8[:, h, :, 1]).then_inc(one_hots_ready, 1)

            def soft_1(q, u):
                dve.wait_ge(top_exp_ready, q + 1)
                if beyond(q, 1):
                    dve.wait_ge(gate_weights_ready, q)
                v.tensor_scalar(den[:, :], ex[:, u % 2, :], 1.0, None, ALU.add).then_inc(softmax_step, 1)

            def soft_2(q, u):
                dve.wait_ge(softmax_step, 2 * q + 1)
                v.reciprocal(st[:, u, :, C_W1], den[:, :]).then_inc(softmax_step, 1)

            def soft_3(q, u):
                dve.wait_ge(softmax_step, 2 * q + 2)
                v.tensor_tensor(st[:, u, :, C_W2], st[:, u, :, C_W1], ex[:, u % 2, :], ALU.mult).then_inc(gate_weights_ready, 1)

            def place_1(q, u):
                h = u % 2
                dve.wait_ge(counts_done, q + 1)
                if beyond(q, 1):
                    dve.wait_ge(places_picked, q)
                v.tensor_tensor(posr[:, h, :, :],
                                ps_agg[h][:, 0:(QUAD + 1) * 2 * NE].rearrange("p (j k) -> p j k", j=QUAD + 1),
                                posr[:, 1 - h, QUAD:QUAD + 1, :].broadcast_to([P, QUAD + 1, 2 * NE]),
                                ALU.add).then_inc(places_ready, 1)

            def place_2(q, u):
                h = u % 2
                dve.wait_ge(places_ready, q + 1)
                if beyond(q, 1):
                    dve.wait_ge(place_ready, q)
                v.tensor_tensor(picked[:, :, :], posr[:, h, 0:QUAD, :].rearrange("p j (r e) -> p (j r) e", r=2),
                                hot[:, h, 2 * NE:].rearrange("p (k e) -> p k e", e=NE), ALU.mult).then_inc(places_picked, 1)

            def place_3(q, u):
                dve.wait_ge(places_picked, q + 1)
                if beyond(q, 1):
                    dve.wait_ge(rows_ready, q)
                v.tensor_reduce(place[:, :, :].rearrange("p j r -> p (j r)"), picked[:, :, :], AX_X,
                                ALU.add).then_inc(place_ready, 1)
                v.tensor_copy(st[:, u, :, C_TOKEN].bitcast(I32), tok[:, bass.ds(QUAD * q, QUAD)])

            def place_4(q, u):
                dve.wait_ge(place_ready, q + 1)
                v.tensor_copy(idx1[:, u, :], place[:, :, 0])
                v.tensor_copy(st[:, u, :, C_RANK2], place[:, :, 1]).then_inc(rows_ready, 1)

            n = [0]

            def link(i):
                n[0] += 1
                i.then_inc(vector_step, 1)
                dve.wait_ge(vector_step, n[0])

            def past(r):
                link(v.tensor_tensor(cmp[:, :, :],
                                     iota_i[0:1, :].rearrange("p (i o) -> p i o", o=1).broadcast_to([1, NIT, NE]),
                                     iend[0:1, r, :].rearrange("p (o e) -> p o e", o=1).broadcast_to([1, NIT, NE]),
                                     ALU.is_ge))

            quads(dve, stats, SLOTS)
            dve.wait_ge(weights_in_front, 16 * 6)
            dve.wait_ge(w2_loaded, 16 * 4)
            B = 3 * NE
            link(v.memset(b2s[:, :], 0.0))
            link(v.tensor_reduce(b2m[0:B, :], b2k[0:B, :], AX_X, ALU.add))
            link(v.tensor_scalar(b2m[0:B, :], b2m[0:B, :], -1.0 / P, None, ALU.mult))
            link(v.tensor_scalar(b2k[0:B, :], b2k[0:B, :], b2m[0:B, :], None, ALU.add))
            link(v.tensor_copy(b2hi[0:B, :], b2k[0:B, :]))
            link(v.tensor_tensor(b2k[0:B, :], b2k[0:B, :], b2hi[0:B, :], ALU.subtract))
            link(v.tensor_copy(b2mid[0:B, :], b2k[0:B, :]))
            link(v.tensor_tensor(b2k[0:B, :], b2k[0:B, :], b2mid[0:B, :], ALU.subtract))
            link(v.tensor_copy(b2lo[0:B, :], b2k[0:B, :]))
            link(v.tensor_copy(b2s[0:B, :], b2lo[0:B, :]))
            link(v.tensor_copy(b2s[0:2 * NE, :], b2mid[0:2 * NE, :]))
            link(v.tensor_copy(b2s[0:NE, :], b2hi[0:NE, :]))

            dve.wait_ge(routing_ready, 1)
            link(v.memset(hot[:, :, 0:2 * NE], 0.0))

            w2v = W2[:, :, :, :].rearrange("p e c f -> p (e c) f")

            def centre_1(q, u):
                if beyond(q, 1):
                    dve.wait_ge(w2_centred, 3 * q)
                v.tensor_reduce(w2m[:, :], w2v[:, bass.ds(q, 1), :], AX_X, ALU.add).then_inc(w2_centred, 1)

            def centre_2(q, u):
                dve.wait_ge(w2_centred, 3 * q + 1)
                v.tensor_scalar(w2m[:, :], w2m[:, :], -1.0 / P, None, ALU.mult).then_inc(w2_centred, 1)

            def centre_3(q, u):
                dve.wait_ge(w2_centred, 3 * q + 2)
                w = w2v[:, bass.ds(q, 1), :].rearrange("p o f -> p (o f)")
                v.tensor_scalar(w, w, w2m[:, :], None, ALU.add).then_inc(w2_centred, 1)

            def turn(q, u):
                def part(does, lag):
                    if beyond(q, lag) and not (isinstance(q, int) and q - lag >= NQ):
                        does(q - lag, (u - lag) % SLOTS)
                part(tile_a, 1)
                part(soft_1, 3)
                part(tile_b, 1)
                part(soft_2, 3)
                part(place_1, 3)
                part(tile_b2, 1)
                part(place_2, 3)
                part(soft_3, 3)
                part(tile_b3, 1)
                part(gate_1, 2)
                part(place_3, 3)
                part(gate_2, 2)
                part(place_4, 3)
                part(gate_3, 2)
                part(centre_1, 0)
                part(gate_4, 2)
                part(centre_2, 0)
                part(gate_5, 2)
                part(centre_3, 0)
            quads(dve, turn, SLOTS)
            for q in range(NQ, NQ + 3):
                turn(q, q % SLOTS)

            dve.wait_ge(rows_ready, NQ)
            final = posr[:, (NQ - 1) % 2, QUAD, :]
            v.tensor_copy(padi[:, :], final[0:1, 0:NE]).then_inc(ends_known, 1)
            link(v.memset(zeros[:, :], 0.0))
            link(v.tensor_tensor(cnt[:, :], final, base[:, :], ALU.subtract))
            link(v.tensor_scalar(cnti[:, :], cnt[:, :], float(P - 1), None, ALU.add))
            link(v.tensor_scalar(nbi[:, :], cnti[:, :], 7, None, ALU.arith_shift_right))
            link(v.tensor_copy(nb[:, :, :].rearrange("p r e -> p (r e)"), nbi[:, :]))
            for r in range(2):
                link(v.tensor_tensor_scan(iend[:, r, :], nb[:, r, :], zeros[:, :], 0.0, ALU.add, ALU.add))
            link(v.tensor_scalar(stride1[:, :], nb[:, 0, :], -1.0, float(CAP // P + SHIFT), ALU.mult, ALU.add))
            past(0)
            link(v.tensor_tensor(cmp[:, :, :], cmp[:, :, :],
                                 stride1[0:1, :].rearrange("p (o e) -> p o e", o=1).broadcast_to([1, NIT, NE]),
                                 ALU.mult))
            link(v.tensor_reduce(etf[:, :], cmp[:, :, :], AX_X, ALU.add))
            link(v.tensor_tensor(etf[:, :], etf[:, :], iota_i[0:1, :], ALU.add))
            link(v.tensor_scalar(etf[:, :], etf[:, :], 2.0, None, ALU.add))
            link(v.tensor_copy(vi[:, :], etf[:, :]))
            link(v.tensor_scalar(sti[:, :], vi[:, :], SHIFT - 1, None, ALU.bitwise_and))
            link(v.tensor_scalar(vi[:, :], vi[:, :], SHIFT.bit_length() - 1, None, ALU.arith_shift_right))
            link(v.tensor_scalar(vi[:, :], vi[:, :], NE - 1, None, ALU.min))
            link(v.tensor_copy(et_pe[:, 0, :], vi[:, :]))
            link(v.tensor_copy(et_act[:, 0, 0:NIT - 2], vi[:, 2:NIT]))
            link(v.tensor_scalar(etf[:, :], sti[:, :], 2.0, None, ALU.subtract))
            link(v.tensor_scalar(sti[:, 0:NIT - 2], etf[:, 2:NIT], float(P), None, ALU.mult))
            link(v.tensor_tensor(start2[:, :], iend[:, 1, :], nb[:, 1, :], ALU.subtract))
            v.tensor_scalar(start2[:, :], start2[:, :], float(P), None, ALU.mult).then_inc(tables_ready, 1)

        front.close()

        mine = sb("mine", [P, QUAD, NE])
        mine2 = sb("mine2", [P, QUAD])
        R = sb("R", [P, RING, QUAD, W_B])
        xT = sb("xT", [P, 2, QUAD * P])
        wr = sb("wr", [P, 2, QUAD, F + 2])
        hs = sb("hs", [P, 2, 2, 2 * P])
        fst = sb("fst", [P, QUAD, 6])
        fmv = sb("fmv", [P, QUAD, 2])
        fve = sb("fve", [P, QUAD])
        fsd = sb("fsd", [P, QUAD])
        frs = sb("frs", [P, QUAD])


        out_rows = out.rearrange("b l d -> (b l) d")
        qb = dram_b.ap().rearrange("(q j p) w -> p q j w", p=P, j=QUAD)
        ps_z, ps_h, ps_o = bank[0], (bank[1:3], bank[3:5]), bank[5:7]

        scrap = sb("scrap", [P, 1])

        def loads_of(r, G, u):
            if r == 0:
                return 64 * (G - u) // RING + 64
            return 64 * NQUAD // RING + 16 * (G - NQUAD - u) // RING + 16

        with nc.Block() as block:
            def passes(eng, body):
                for r in range(2):
                    n = NQUAD // RING
                    for u in range(RING):
                        body(r, u, u + NQUAD * r, u, False)
                    with eng.Fori(1, n - 1) as J:
                        for u in range(RING):
                            body(r, RING * J + u, RING * J + u + NQUAD * r, u, False)
                    for u in range(RING):
                        q = NQUAD - RING + u
                        body(r, q, q + NQUAD * r, u, u == RING - 1)

            @block.sync
            def _(sp):
                def quad(r, q, G, u, last):
                    if not (isinstance(G, int) and G < RING):
                        sp.wait_ge(blocks_sent[u], 64 * (G - u) // RING)
                    if r == 0:
                        rows = numbers(sp, sti[0:1, bass.ds(QUAD * q, QUAD)], ROWS_A - P)
                        for j, row in enumerate(rows):
                            sp.dma_start(R[:, u, j, 0:W_A], dram_a.ap()[bass.ds(row, P), :]).then_inc(blocks_loaded[u], 16)
                    else:
                        sp.dma_start(R[:, u, :, :], qb[:, bass.ds(q, 1), :, :].rearrange("p o j w -> p (o j) w")
                                     ).then_inc(blocks_loaded[u], 16)

                sp.wait_ge(tables_ready, 1)
                for u in range(SLOTS):
                    sp.wait_ge(rows_sent[u], 64 * NQ // SLOTS)
                sp.wait_ge(surplus_filled, 16)
                sp.wait_ge(padded, 16 * NE)
                for r in range(2):
                    if r == 0:
                        for u in range(RING):
                            quad(r, u, u, u, False)
                    else:
                        for u in range(RING):
                            sp.wait_ge(blocks_sent[u], 64 * NQUAD // RING)
                    with sp.Fori(1 - r, NQUAD // RING) as J:
                        for u in range(RING):
                            quad(r, RING * J + u, RING * J + u + NQUAD * r, u, False)
                for u in range(RING):
                    sp.wait_ge(blocks_sent[u], 64 * 2 * NQUAD // RING)

            @block.gpsimd
            def _(pool):
                g = nc.gpsimd
                pool.wait_ge(second_filled, 16 * 6)

                def quad(r, q, G, u, last):
                    for j in range(QUAD):
                        if r == 0:
                            if j == 0:
                                hold(pool, x1_beta_ready, G + 1)
                            if j % 2 == 0:
                                hold(pool, share_added, 2 * G + j // 2 + 1)
                            scatter(dram_b.ap(), R[:, u, j, C_POS2:C_POS2 + 1].bitcast(I32), R[:, u, j, :],
                                    NBLK * P).then_inc(blocks_sent[u], 16)
                        else:
                            if j == 0:
                                hold(pool, result_ready, G - NQUAD + 1)
                            scatter(out_rows, R[:, u, j, C_TOKEN:C_TOKEN + 1].bitcast(I32), R[:, u, j, C_Y:W_B],
                                    P * P).then_inc(blocks_sent[u], 16)
                passes(pool, quad)

            @block.tensor
            def _(pe):
                mm = nc.tensor.matmul
                pe.wait_ge(w1_loaded, 16 * 5)
                pe.wait_ge(pool_built, 9)
                pe.wait_ge(w2_centred, 3 * NQ)
                pe.wait_ge(tables_ready, 1)

                def turn(r, G, u):
                    if r:
                        pe.wait_ge(blocks_loaded[u], loads_of(r, G, u))
                    else:
                        pe.wait_ge(z_ready, G + 1)
                    if not (isinstance(G, int) and G < 1):
                        pe.wait_ge(zT_ready, G)
                    for j in range(QUAD):
                        i = nc.tensor.transpose(ps_z[:, j * P:(j + 1) * P], R[:, u, j, C_Z:C_Y],
                                                ident[:, :])
                    i.then_inc(z_turned, 1)

                def first(G, u, h):
                    if h == 0:
                        pe.wait_ge(zT_ready, G + 1)
                    pe.wait_ge(w1_copied, 2 * G + h + 1)
                    for c in range(2):
                        for j in range(2 * h, 2 * h + 2):
                            i = mm(ps_h[c][h][:, (j % 2) * P:(j % 2 + 1) * P], wr[:, u % 2, j, c * P:(c + 1) * P],
                                   xT[:, u % 2, j * P:(j + 1) * P], start=True, stop=True)
                    i.then_inc(hidden_done, 1)

                def second(r, G, h, e):
                    n = 2 * G + h
                    if not (isinstance(G, int) and G < 1):
                        pe.wait_ge(share_added, n - 1)
                    if not r:
                        pe.wait_ge(relu0_done, n + 1)
                    pe.wait_ge(relu1_done, n + 1)
                    for k in range(2):
                        o = ps_o[h][:, k * P:(k + 1) * P]
                        mm(o, sel[:, bass.ds(e[k], 1), :].rearrange("p o m -> p (o m)"), b2s[:, :], start=True,
                           stop=False, skip_group_check=True)
                        for c in range(2):
                            i = mm(o, hs[:, h, c, k * P:(k + 1) * P],
                                   W2[:, bass.ds(e[k], 1), c, :].rearrange("p o f -> p (o f)"), start=False,
                                   stop=c == 1, skip_group_check=True)
                    i.then_inc(output_done, 1)

                def experts(r, q):
                    return numbers(pe, et_pe[0:1, r, bass.ds(QUAD * q, QUAD)])

                def quad(r, q, G, u, last):
                    start = isinstance(q, int) and q == 0
                    if start:
                        turn(r, G, u)
                    first(G, u, 0)
                    if start:
                        pe.wait_ge(tables_ready, r + 1)
                    e = experts(r, q)
                    if not start:
                        second(r, G - 1, 1, e[0:2])
                    first(G, u, 1)
                    if not last:
                        turn(r, G + 1, (u + 1) % RING)
                    second(r, G, 0, e[2:4])
                    if last:
                        second(r, G, 1, experts(r, q + 1))
                passes(pe, quad)

            @block.scalar
            def _(act):
                a = nc.scalar.activation
                act.wait_ge(tables_ready, 1)
                act.wait_ge(w1_loaded, 16 * 5)

                def turn_out(G, u):
                    act.wait_ge(z_turned, G + 1)
                    nc.scalar.copy(xT[:, u % 2, :], ps_z[:, :]).then_inc(zT_ready, 1)

                def weights(r, q, G, u, j, e):
                    if j == 0 and not (isinstance(G, int) and G < 2):
                        act.wait_ge(hidden_done, 2 * G - 2)
                        if r == 0 or (isinstance(q, int) and q < 2):
                            act.wait_ge(relu0_done, 2 * G - 2)
                        act.wait_ge(relu1_done, 2 * G - 2)
                    i = nc.scalar.copy(wr[:, u % 2, j, :], W1b[:, bass.ds(e, 1), :].rearrange("p o f -> p (o f)"))
                    if j % 2:
                        i.then_inc(w1_copied, 1)

                def relu(r, G, u, h):
                    n = 2 * G + h
                    act.wait_ge(hidden_done, n + 1)
                    if not (isinstance(G, int) and G < 1):
                        act.wait_ge(output_done, n - 1)
                    for c in range(2) if r else range(1, 2):
                        for k in range(2):
                            i = a(hs[:, h, c, k * P:(k + 1) * P], ps_h[c][h][:, k * P:(k + 1) * P], ACT.Relu,
                                  bias=wr[:, u % 2, 2 * h + k, F + c:F + c + 1])
                    i.then_inc(relu1_done, 1)

                def root(G):
                    n = G - NQUAD
                    act.wait_ge(y_var_ready, n + 1)
                    if not (isinstance(n, int) and n < 1):
                        act.wait_ge(y_rstd_ready, n)
                    a(fsd[:, :], fve[:, :], ACT.Sqrt).then_inc(y_std_ready, 1)

                def experts(r, q):
                    return numbers(act, et_act[0:1, r, bass.ds(QUAD * q, QUAD)])

                def quad(r, q, G, u, last):
                    start = isinstance(q, int) and q == 0
                    if start:
                        act.wait_ge(tables_ready, r + 1)
                        for j, e in enumerate(experts(r, q)):
                            weights(r, q, G, u, j, e)
                        turn_out(G, u)
                    e = None if last else experts(r, q + 1)
                    v = (u + 1) % RING
                    relu(r, G, u, 0)
                    if not last:
                        weights(r, q + 1, G + 1, v, 0, e[0])
                        weights(r, q + 1, G + 1, v, 1, e[1])
                    relu(r, G, u, 1)
                    if not last:
                        turn_out(G + 1, v)
                        weights(r, q + 1, G + 1, v, 2, e[2])
                        weights(r, q + 1, G + 1, v, 3, e[3])
                    if r == 1 and not start:
                        root(G - 1)
                    if last and r == 1:
                        root(G)
                passes(act, quad)

            @block.vector
            def _(dve):
                v = nc.vector
                dve.wait_ge(w1_loaded, 16 * 5)

                def zed(r, G, u):
                    dve.wait_ge(blocks_loaded[u], loads_of(r, G, u))
                    for j in range(QUAD):
                        i = v.tensor_scalar(R[:, u, j, C_Z:C_Y], R[:, u, j, 0:P],
                                            R[:, u, j, C_RSTD:C_RSTD + 1], R[:, u, j, C_NMR:C_NMR + 1],
                                            ALU.mult, ALU.add)
                    i.then_inc(z_ready, 1)

                def relu(G, u, h):
                    n = 2 * G + h
                    dve.wait_ge(hidden_done, n + 1)
                    if not (isinstance(G, int) and G < 1):
                        dve.wait_ge(output_done, n - 1)
                    for k in range(2):
                        i = v.tensor_scalar(hs[:, h, 0, k * P:(k + 1) * P], ps_h[0][h][:, k * P:(k + 1) * P],
                                            wr[:, u % 2, 2 * h + k, F:F + 1], 0.0, ALU.add, ALU.max)
                    i.then_inc(relu0_done, 1)

                def share(r, G, u, h):
                    dve.wait_ge(output_done, 2 * G + h + 1)
                    w = C_W2 if r else C_W1
                    for k in range(2):
                        j = 2 * h + k
                        y = R[:, u, j, C_Y:W_B]
                        i = v.scalar_tensor_tensor(out=y, in0=ps_o[h][:, k * P:(k + 1) * P],
                                                   scalar=R[:, u, j, w:w + 1],
                                                   in1=y if r else R[:, u, j, C_Z:C_Y], op0=ALU.mult,
                                                   op1=ALU.add)
                    i.then_inc(share_added, 1)

                def norm_a(G, u):
                    m = G - NQUAD
                    hold(dve, share_added, 2 * G + 2)
                    for j in range(QUAD):
                        i = v.bn_stats(fst[:, j, :], R[:, u, j, C_Y:W_B])
                    i.then_inc(y_stats, 1)
                    hold(dve, y_stats, m + 1)
                    v.memset(scrap[:, :], 0.0)
                    for j in range(QUAD):
                        i = v.bn_aggr(fmv[:, j, :], fst[:, j, :])
                    i.then_inc(y_moments, 1)
                    dve.wait_ge(y_moments, m + 1)
                    v.tensor_scalar(fve[:, :], fmv[:, :, 1], LN_EPS, None, ALU.add).then_inc(y_var_ready, 1)

                def norm_b(G, u):
                    m = G - NQUAD
                    y = R[:, u, :, C_Y:W_B]
                    v.tensor_tensor(y, y, gm_bc[:, :].rearrange("p (o d) -> p o d", o=1).broadcast_to([P, QUAD, P]),
                                    ALU.mult).then_inc(y_scaled, 1)
                    dve.wait_ge(y_std_ready, m + 1)
                    v.reciprocal(frs[:, :], fsd[:, :]).then_inc(y_rstd_ready, 1)
                    dve.wait_ge(y_rstd_ready, m + 1)
                    dve.wait_ge(y_scaled, m + 1)
                    for j in range(QUAD):
                        y = R[:, u, j, C_Y:W_B]
                        i = v.scalar_tensor_tensor(out=y, in0=y, scalar=frs[:, j:j + 1], in1=R[:, u, j, 0:P],
                                                   op0=ALU.mult, op1=ALU.add)
                    i.then_inc(result_ready, 1)

                def add_beta(G, u):
                    if not (isinstance(G, int) and G < 1):
                        dve.wait_ge(second_step, 3 * G)
                        dve.wait_ge(x1_beta_ready, G)
                    v.tensor_tensor(mine[:, :, :], R[:, u, :, C_E2:C_E2 + 1].broadcast_to([P, QUAD, NE]),
                                    iota_e[:, 0:QUAD * NE].rearrange("p (j e) -> p j e", j=QUAD),
                                    ALU.is_equal).then_inc(second_step, 1)
                    dve.wait_ge(second_step, 3 * G + 1)
                    v.tensor_tensor(mine[:, :, :], mine[:, :, :],
                                    start2[:, :].rearrange("p (o e) -> p o e", o=1).broadcast_to([P, QUAD, NE]),
                                    ALU.mult).then_inc(second_step, 1)
                    dve.wait_ge(second_step, 3 * G + 2)
                    v.tensor_reduce(mine2[:, :], mine[:, :, :], AX_X, ALU.add).then_inc(second_step, 1)
                    dve.wait_ge(second_step, 3 * G + 3)
                    v.tensor_tensor(R[:, u, :, C_POS2].bitcast(I32), mine2[:, :], R[:, u, :, C_RANK2], ALU.add)
                    dve.wait_ge(z_ready, G + 1)
                    x1 = R[:, u, :, 0:P]
                    v.tensor_tensor(x1, x1, bt_bc[:, :].rearrange("p (o d) -> p o d", o=1).broadcast_to([P, QUAD, P]),
                                    ALU.add).then_inc(x1_beta_ready, 1)

                def quad(r, q, G, u, last):
                    start = isinstance(q, int) and q == 0
                    before = (u - 1) % RING
                    if start and r == 0:
                        zed(r, G, u)
                    if not last and r == 0:
                        zed(r, G + 1, (u + 1) % RING)
                    if not r:
                        relu(G, u, 0)
                    if not start:
                        share(r, G - 1, before, 1)
                        if r:
                            norm_a(G - 1, before)
                    if not r:
                        relu(G, u, 1)
                        add_beta(G, u)
                    share(r, G, u, 0)
                    if r and not start:
                        norm_b(G - 1, before)
                    if last:
                        share(r, G, u, 1)
                        if r:
                            norm_a(G, u)
                            norm_b(G, u)
                        else:
                            v.tensor_tensor(cmp[:, :, :],
                                            iota_i[0:1, :].rearrange("p (i o) -> p i o", o=1)
                                            .broadcast_to([1, NIT, NE]),
                                            iend[0:1, 1, :].rearrange("p (o e) -> p o e", o=1)
                                            .broadcast_to([1, NIT, NE]), ALU.is_ge).then_inc(table_step, 1)
                            dve.wait_ge(table_step, 1)
                            v.tensor_reduce(etf[:, :], cmp[:, :, 0:NE - 1], AX_X, ALU.add).then_inc(table_step, 1)
                            dve.wait_ge(table_step, 2)
                            v.tensor_copy(et_pe[:, 1, :], etf[:, :])
                            v.tensor_copy(et_act[:, 1, 0:NIT - 2], etf[:, 2:NIT]).then_inc(tables_ready, 1)
                passes(dve, quad)


_INS = ['x', 'adj', 'L0_gnn_e_weight', 'L0_gnn_Wx', 'L0_gnn_Wh', 'L0_gnn_b', 'L0_ffn_gate_w', 'L0_ffn_gate_b',
        'L0_ffn_w1', 'L0_ffn_b1', 'L0_ffn_w2', 'L0_ffn_b2', 'L0_ffn_gamma', 'L0_ffn_beta']


def kernel(**inputs):
    import numpy as _np
    import concourse.bacc as _bacc
    from concourse import mybir as _mybir
    from concourse.bass_utils import run_bass_kernel_spmd as _run

    nc = _bacc.Bacc("TRN2", target_bir_lowering=False, num_devices=1)
    arrays, args = {}, []
    for name in _INS:
        a = _np.ascontiguousarray(inputs[name])
        arrays[f"in_{name}_dram"] = a
        args.append(nc.dram_tensor(f"in_{name}_dram", a.shape, _mybir.dt.from_np(a.dtype), kind="ExternalInput").ap())
    args.append(nc.dram_tensor("out_0_dram", inputs['x'].shape, F32, kind="ExternalOutput").ap())
    build(nc, *args)
    r = _run(nc, [arrays], core_ids=[0])
    return r.results[0]["out_0_dram"]
```
